# Optimizing a Trainium2 kernel written in Bass

```python
import numpy as np
import jax
import jax.numpy as jnp

def _softmax(x, axis=-1):
    return jax.nn.softmax(x, axis=axis)

def _gelu(x):
    return jax.nn.gelu(x, approximate=True)

def _silu(x):
    return jax.nn.silu(x)

def _sigmoid(x):
    return jax.nn.sigmoid(x)

def _layernorm(x, axis=-1, eps=1e-05):
    m = jnp.mean(x, axis=axis, keepdims=True)
    v = jnp.var(x, axis=axis, keepdims=True)
    return (x - m) / jnp.sqrt(v + eps)

def _scatter_add(tgt, idx, src, axis=0):
    return tgt.at[idx].add(src)

def _segment_sum(src, seg, n):
    return jax.ops.segment_sum(src, seg, n)
kernel_name = 'mk_macaron_d1_jaxref_r8_3f96a9'

def setup_inputs(seed: int=0):
    np.random.seed(seed)
    _w = jnp.asarray

    def _L0_attn_setup():
        import jax, jax.numpy as jnp
        import numpy as np
        B, T, D = (8, 256, 128)
        H, N = (8, 32)

        def _xavier(key, shape, fan_in, fan_out):
            lim = float(np.sqrt(6.0 / (fan_in + fan_out)))
            return jax.random.uniform(key, shape, jnp.float32, -lim, lim)

        def _reference_tuple_inner(x, W_in, W_k, W_v, W_q, W_beta, b_beta, W_out):
            b, t, d = x.shape
            h, n = b_beta.shape
            xp = jax.nn.silu(jnp.einsum('btd,ed->bte', x, W_in))

            def proj(W):
                return jnp.einsum('btd,md->btm', xp, W).reshape(b, t, h, n).transpose(1, 0, 2, 3)
            k_all = proj(W_k)
            v_all = proj(W_v)
            q_all = proj(W_q)
            beta_all = jax.nn.sigmoid(proj(W_beta) + b_beta)
            S0 = jnp.zeros((b, h, n, n), x.dtype)

            def step(S, inp):
                k, v, q, beta = inp
                kn = k / (jnp.linalg.norm(k, axis=-1, keepdims=True) + 1e-06)
                retrieved = jnp.einsum('bhij,bhj->bhi', S, kn)
                delta = v - retrieved
                S = jnp.tanh(beta[..., None] * S + delta[..., None] * kn[..., None, :])
                Sq = jnp.einsum('bhij,bhj->bhi', S, q)
                out = Sq * jax.nn.silu(Sq)
                return (S, out)
            S_final, outs = jax.lax.scan(step, S0, (k_all, v_all, q_all, beta_all))
            cell_out = outs.transpose(1, 0, 2, 3).reshape(b, t, h * n)
            y = jnp.einsum('btm,dm->btd', cell_out, W_out)
            return (y, S_final)
        key = jax.random.key(seed)
        ks = jax.random.split(key, 8)
        x = jax.random.normal(ks[0], (B, T, D), jnp.float32)
        W_in = _xavier(ks[1], (D, D), D, D)
        W_k = _xavier(ks[2], (H * N, D), N, D)
        W_v = _xavier(ks[3], (H * N, D), N, D)
        W_q = _xavier(ks[4], (H * N, D), N, D)
        W_beta = _xavier(ks[5], (H * N, D), N, D)
        b_beta = jnp.full((H, N), 2.0, jnp.float32)
        W_out = _xavier(ks[6], (D, H * N), H * N, D)
        return {'x': x, 'W_in': W_in, 'W_k': W_k, 'W_v': W_v, 'W_q': W_q, 'W_beta': W_beta, 'b_beta': b_beta, 'W_out': W_out}
    _L0_attn_in = _L0_attn_setup()

    def _L0_ffn_setup():
        import jax, jax.numpy as jnp
        import numpy as np
        TOP_K = 8
        key = jax.random.key(seed)
        ks = jax.random.split(key, 6)
        B, S, D, F, E = (2, 128, 128, 64, 64)
        x = jax.random.normal(ks[0], (B, S, D), dtype=jnp.float32)
        centroids = jax.random.normal(ks[1], (E, D), dtype=jnp.float32) * 0.05
        expert_biases = jnp.zeros((E,), dtype=jnp.float32)
        Ws_up = jax.random.normal(ks[2], (D, F), dtype=jnp.float32) / np.sqrt(D)
        Ws_down = jax.random.normal(ks[3], (F, D), dtype=jnp.float32) / np.sqrt(F)
        W_up = jax.random.normal(ks[4], (E, D, F), dtype=jnp.float32) / np.sqrt(D)
        W_down = jax.random.normal(ks[5], (E, F, D), dtype=jnp.float32) / np.sqrt(F)
        return {'x': x, 'centroids': centroids, 'expert_biases': expert_biases, 'Ws_up': Ws_up, 'Ws_down': Ws_down, 'W_up': W_up, 'W_down': W_down}
    _L0_ffn_in = _L0_ffn_setup()
    _d = {'L0_attn_x': _L0_attn_in['x'], 'L0_attn_W_in': _L0_attn_in['W_in'], 'L0_attn_W_k': _L0_attn_in['W_k'], 'L0_attn_W_v': _L0_attn_in['W_v'], 'L0_attn_W_q': _L0_attn_in['W_q'], 'L0_attn_W_beta': _L0_attn_in['W_beta'], 'L0_attn_b_beta': _L0_attn_in['b_beta'], 'L0_attn_W_out': _L0_attn_in['W_out'], 'L0_ffn_centroids': _L0_ffn_in['centroids'], 'L0_ffn_expert_biases': _L0_ffn_in['expert_biases'], 'L0_ffn_Ws_up': _L0_ffn_in['Ws_up'], 'L0_ffn_Ws_down': _L0_ffn_in['Ws_down'], 'L0_ffn_W_up': _L0_ffn_in['W_up'], 'L0_ffn_W_down': _L0_ffn_in['W_down']}
    _x0 = _d['L0_attn_x']
    _d['L0_attn_x'] = jax.random.normal(jax.random.fold_in(jax.random.key(seed), 1), (2, 1024, 128), dtype=_x0.dtype)
    del _x0
    return _d

def reference(L0_attn_x, L0_attn_W_in, L0_attn_W_k, L0_attn_W_v, L0_attn_W_q, L0_attn_W_beta, L0_attn_b_beta, L0_attn_W_out, L0_ffn_centroids, L0_ffn_expert_biases, L0_ffn_Ws_up, L0_ffn_Ws_down, L0_ffn_W_up, L0_ffn_W_down):

    def _L0_attn_ref(x, W_in, W_k, W_v, W_q, W_beta, b_beta, W_out):
        import jax, jax.numpy as jnp
        import numpy as np
        B, T, D = (8, 256, 128)
        H, N = (8, 32)

        def _xavier(key, shape, fan_in, fan_out):
            lim = float(np.sqrt(6.0 / (fan_in + fan_out)))
            return jax.random.uniform(key, shape, jnp.float32, -lim, lim)

        def _reference_tuple_inner(x, W_in, W_k, W_v, W_q, W_beta, b_beta, W_out):
            b, t, d = x.shape
            h, n = b_beta.shape
            xp = jax.nn.silu(jnp.einsum('btd,ed->bte', x, W_in))

            def proj(W):
                return jnp.einsum('btd,md->btm', xp, W).reshape(b, t, h, n).transpose(1, 0, 2, 3)
            k_all = proj(W_k)
            v_all = proj(W_v)
            q_all = proj(W_q)
            beta_all = jax.nn.sigmoid(proj(W_beta) + b_beta)
            S0 = jnp.zeros((b, h, n, n), x.dtype)

            def step(S, inp):
                k, v, q, beta = inp
                kn = k / (jnp.linalg.norm(k, axis=-1, keepdims=True) + 1e-06)
                retrieved = jnp.einsum('bhij,bhj->bhi', S, kn)
                delta = v - retrieved
                S = jnp.tanh(beta[..., None] * S + delta[..., None] * kn[..., None, :])
                Sq = jnp.einsum('bhij,bhj->bhi', S, q)
                out = Sq * jax.nn.silu(Sq)
                return (S, out)
            S_final, outs = jax.lax.scan(step, S0, (k_all, v_all, q_all, beta_all))
            cell_out = outs.transpose(1, 0, 2, 3).reshape(b, t, h * n)
            y = jnp.einsum('btm,dm->btd', cell_out, W_out)
            return (y, S_final)
        return _reference_tuple_inner(x, W_in, W_k, W_v, W_q, W_beta, b_beta, W_out)[0]

    def _L0_ffn_ref(x, centroids, expert_biases, Ws_up, Ws_down, W_up, W_down):
        import jax, jax.numpy as jnp
        import numpy as np
        TOP_K = 8
        B, S, D = x.shape
        E = centroids.shape[0]
        T = B * S
        xf = x.reshape(T, D)
        shared = jax.nn.silu(xf @ Ws_up) @ Ws_down
        aff = xf @ centroids.T
        biased = aff + expert_biases
        _, idx = jax.lax.top_k(biased, TOP_K)
        sel = jnp.take_along_axis(aff, idx, axis=1)
        w = jax.nn.sigmoid(sel)
        w = w / (jnp.sum(w, axis=-1, keepdims=True) + 1e-08)
        cw = jnp.zeros((T, E), dtype=x.dtype).at[jnp.arange(T)[:, None], idx].add(w)
        h = jax.nn.silu(jnp.einsum('td,edf->etf', xf, W_up))
        y = jnp.einsum('etf,efd->etd', h, W_down)
        routed = jnp.einsum('etd,te->td', y, cw)
        return (shared + routed).reshape(B, S, D)
    x = L0_attn_x
    x = x + 0.5 * _L0_ffn_ref(_layernorm(x, axis=-1), L0_ffn_centroids, L0_ffn_expert_biases, L0_ffn_Ws_up, L0_ffn_Ws_down, L0_ffn_W_up, L0_ffn_W_down)
    x = x + _L0_attn_ref(_layernorm(x, axis=-1), L0_attn_W_in, L0_attn_W_k, L0_attn_W_v, L0_attn_W_q, L0_attn_W_beta, L0_attn_b_beta, L0_attn_W_out)
    x = x + 0.5 * _L0_ffn_ref(_layernorm(x, axis=-1), L0_ffn_centroids, L0_ffn_expert_biases, L0_ffn_Ws_up, L0_ffn_Ws_down, L0_ffn_W_up, L0_ffn_W_down)
    return x

_drawn_inputs = setup_inputs


def setup_inputs(seed=0):
    import zlib

    import numpy as np

    out = dict(_drawn_inputs(seed))
    spreads = {'L0_attn_b_beta': (2.0, 0.2), 'L0_ffn_expert_biases': (0.0, 0.1)}
    factors = {}
    for name, (base, spread) in spreads.items():
        noise = np.random.default_rng([zlib.crc32(name.encode()), seed]).standard_normal(out[name].shape)
        drawn = base * np.exp(spread * noise) if base else spread * noise
        out[name] = jnp.asarray(drawn.astype(out[name].dtype))
    for name, factor in factors.items():
        out[name] = (out[name] * factor).astype(out[name].dtype)
    return out
```

```python
from contextlib import ExitStack

import concourse.bass as bass
from concourse import mybir

F32 = mybir.dt.float32
ALU = mybir.AluOpType
ACT = mybir.ActivationFunctionType
AX = mybir.AxisListType

P = 128
D = 128
HEADS, N = 8, 32
M = HEADS * N
E, F = 64, 64
EC = E * F // P
B, T = 2, 1024
STEPS = 64
TILES = T // STEPS
G = 4
GRP = 16
NGRP = STEPS // GRP
RING = 32
HALF = STEPS // 2
W1 = N + 1
LN_EPS, NORM_EPS, SUM_EPS = 1e-5, 1e-6, 1e-8
CH = EC + 1

GD, GT, GA = 13, 3, 3
PD, PP, PT, PA = 9, 2, 3, 7
BCAST = 0


def macaron_program(nc, x, w_in, w_k, w_v, w_q, w_beta, b_beta, w_out, cent, ebias, ws_up, ws_down, w_up, w_down,
                    out, key_rows, query_rows):
    with ExitStack() as ctx:
        def sb(name, shape):
            return ctx.enter_context(nc.sbuf_tensor(name, shape, F32))

        def ps(name):
            return ctx.enter_context(nc.psum_tensor(name, [P, 512], F32))

        def sem(name):
            return ctx.enter_context(nc.semaphore(name))

        WU = sb("WU", [P, EC, 2, F])
        WD = sb("WD", [P, EC, D])
        WSU = sb("WSU", [P, F])
        WSD = sb("WSD", [F, D])
        CENT = sb("CENT", [P, E])
        EB = sb("EB", [P, E])
        WIN = sb("WIN", [P, D])
        WK = sb("WK", [P, M])
        WQ = sb("WQ", [P, M])
        WV = sb("WV", [P, M])
        WB = sb("WB", [P, M])
        WO = sb("WO", [P, 2, D])
        BB = sb("BB", [P, 2])
        IDENT = sb("IDENT", [P, P])
        SEL = sb("SEL", [E, E, F])
        POW = sb("POW", [P, 16])
        XA = sb("XA", [P, D])
        X1N = sb("X1N", [P, D])
        X1P = sb("X1P", [P, D])
        X2 = sb("X2", [P, D])
        OT = sb("OT", [P, D])
        XT = sb("XT", [P, 2, P])
        CT = sb("CT", [E, 2, P])
        HS = sb("HS", [P, 2, 2, P])
        HG = sb("HG", [P, 2, 2, P])
        HSH = sb("HSH", [F, 2, P])
        st = [sb(f"st{u}", [P, 6]) for u in range(3)]
        mv = [sb(f"mv{u}", [P, 2]) for u in range(3)]
        ve = [sb(f"ve{u}", [P, 1]) for u in range(3)]
        rstd = [sb(f"rstd{u}", [P, 1]) for u in range(3)]
        xn = [sb(f"xn{u}", [P, D]) for u in range(3)]
        biased = [sb(f"biased{u}", [P, E]) for u in range(2)]
        top8 = [sb(f"top8{u}", [P, 8]) for u in range(2)]
        rest = [sb(f"rest{u}", [P, E]) for u in range(2)]
        chosen = [sb(f"chosen{u}", [P, E]) for u in range(2)]
        th_aff = [sb(f"th_aff{u}", [P, E]) for u in range(2)]
        w2 = [sb(f"w2{u}", [P, E]) for u in range(2)]
        wsum = [sb(f"wsum{u}", [P, 3]) for u in range(2)]
        cw = [sb(f"cw{u}", [P, P]) for u in range(2)]
        XNT = sb("XNT", [P, P])
        XP = sb("XP", [P, P])
        KSQ = sb("KSQ", [P, M])
        KSS = sb("KSS", [P, 4, HEADS])
        KT = sb("KT", [P, HEADS, W1])
        QT = sb("QT", [P, M])
        VN = sb("VN", [P, 2, B, STEPS])
        BN = sb("BN", [P, 2, B, STEPS])
        BT = sb("BT", [P, 2, B, STEPS])
        KB = sb("KB", [P, STEPS, G, W1])
        QB = sb("QB", [P, STEPS, G, N])
        SR = sb("SR", [P, RING, G, W1])
        PR = sb("PR", [P, G, W1])
        DEL = sb("DEL", [P, G])
        WT = sb("WT", [P, G, N])
        QS = sb("QS", [P, G, N])
        UU = sb("UU", [P, G, N])
        PQ = sb("PQ", [P, STEPS, G, N])
        SQS = sb("SQS", [P, STEPS, G])
        CO = sb("CO", [P, 2, B, STEPS])

        up_ps = [ps("up0"), ps("up1")]
        acc = [ps("acc0"), ps("acc1")]
        cell_ps = ps("cell_ps")
        kq_ps = ps("kq_ps")
        vb_ps = ps("vb_ps")
        gate_ps = [ps("gate_ps"), vb_ps]

        weights_in = sem("weights_in")
        pool_consts, dve_consts = sem("pool_consts"), sem("dve_consts")
        x_in = sem("x_in")
        gd = [sem("gd0"), sem("gd1")]
        gp = [sem("gp0"), sem("gp1")]
        gt = [sem("gt0"), sem("gt1")]
        ga = [sem("ga0"), sem("ga1")]
        up_done, silu_done, gated, down_done = sem("up_done"), sem("silu_done"), sem("gated"), sem("down_done")
        x1_done, out_ready, out_stored = sem("x1_done"), sem("out_ready"), sem("out_stored")
        pd, pp, pt, pa = sem("pd"), sem("pp"), sem("pt"), sem("pa")
        k_stored, q_stored, v_placed, beta_placed = (sem(s) for s in ("k_stored", "q_stored", "v_placed", "beta_placed"))
        kb_in = [sem(f"kb_in{r}") for r in range(NGRP)]
        qb_in = [sem(f"qb_in{r}") for r in range(NGRP)]
        prod_done, delta_done, outer_done, u_done, s_done, bs_done, pq_done = (sem(s) for s in (
            "prod_done", "delta_done", "outer_done", "u_done", "s_done", "bs_done", "pq_done"))
        sq_done, osilu_done, co_done, y_done, x2_done = (sem(s) for s in (
            "sq_done", "osilu_done", "co_done", "y_done", "x2_done"))

        carried = sem("carried")

        def each_iteration(eng, body):
            body(0, (True, False, False))
            body(1, (True, True, False))
            with eng.Fori(2, TILES - 1) as k:
                body(k, (True, True, True))
            body(TILES - 1, (True, True, True))
            body(TILES, (False, True, True))
            body(TILES + 1, (False, False, True))

        def g_of(h):
            return slice(2 * h, 2 * h + 2)

        NW = 15
        block = ctx.enter_context(nc.Block())

        @block.sync
        def _(sp):
            sp.dma_start(XA[0:STEPS, :], x[0, 0:STEPS, :]).then_inc(x_in, 16)
            sp.dma_start(XA[STEPS:P, :], x[1, 0:STEPS, :]).then_inc(x_in, 16)
            for dst, src in ((CENT[:], cent), (EB[:], ebias.partition_broadcast(P)), (WSU[:], ws_up), (WSD[:], ws_down),
                             (WU[:], w_up.rearrange("(c m) d f -> d c m f", m=2)),
                             (WD[:], w_down.rearrange("(c m) f d -> (m f) c d", m=2)),
                             (WIN[:], w_in), (WK[:], w_k), (WQ[:], w_q), (WV[:], w_v), (WB[:], w_beta),
                             (WO[:], w_out.rearrange("(h p) d -> p h d", h=2)),
                             (BB[:], b_beta)):
                sp.dma_start(dst, src).then_inc(weights_in, 16)

            def iteration(k, has):
                if has[0]:
                    for b in range(B):
                        if b == 0:
                            sp.wait_ge(pd, k * PD + 8)
                        dst = key_rows.rearrange("s t (b h) w -> b t h s w", b=B)[b]
                        for h in range(2):
                            sp.dma_start(dst[:, h], KT[b * STEPS:(b + 1) * STEPS, 4 * h:4 * h + 4, :]).then_inc(k_stored, 16)
                    for b in range(B):
                        if b == 0:
                            sp.wait_ge(pa, k * PA + 4)
                        dst = query_rows.rearrange("s t (b h) w -> b t h s w", b=B)[b]
                        for h in range(2):
                            sp.dma_start(dst[:, h], QT[b * STEPS:(b + 1) * STEPS, 128 * h:128 * h + 128].rearrange(
                                "t (s w) -> t s w", s=4)).then_inc(q_stored, 16)
                    sp.wait_ge(x1_done, 2 * k + 2)
                    sp.sem_inc(carried, 1)
                    if not isinstance(k, int) or k + 1 < TILES:
                        for b in range(B):
                            sp.dma_start(XA[b * STEPS:(b + 1) * STEPS, :],
                                         x[b, bass.ds((k + 1) * STEPS, STEPS), :]).then_inc(x_in, 16)
                if has[2]:
                    sp.wait_ge(out_ready, k - 1)
                    sp.sem_inc(carried, 1)
                    for b in range(B):
                        sp.dma_start(out[b, bass.ds((k - 2) * STEPS, STEPS), :],
                                     OT[b * STEPS:(b + 1) * STEPS, :]).then_inc(out_stored, 16)
                if has[0]:
                    sp.wait_ge(k_stored, 64 * (k + 1))
                    sp.wait_ge(q_stored, 64 * (k + 1))
                    for r in range(NGRP):
                        if has[1]:
                            sp.wait_ge(pq_done, (k - 1) * STEPS + GRP * (r + 1))
                        for s in range(4):
                            rows = slice(N * s, N * s + N)
                            steps = slice(GRP * r, GRP * r + GRP)
                            sp.dma_start(KB[rows, steps, :, :].rearrange("p t g w -> p (t g w)"),
                                         key_rows[s, steps].rearrange("t g w -> (t g w)").partition_broadcast(N)).then_inc(kb_in[r], 16)
                            sp.dma_start(QB[rows, steps, :, :].rearrange("p t g w -> p (t g w)"),
                                         query_rows[s, steps].rearrange("t g w -> (t g w)").partition_broadcast(N)).then_inc(qb_in[r], 16)
                    for r in range(NGRP):
                        sp.wait_ge(kb_in[r], 64 * (k + 1))
                        sp.wait_ge(qb_in[r], 64 * (k + 1))
                    sp.sem_inc(carried, 1)

            each_iteration(sp, iteration)
            sp.wait_ge(out_stored, 32 * TILES)

        @block.gpsimd
        def _(pool):
            pool.memset(IDENT[:], 0.0).then_inc(pool_consts, 1)
            pool.memset(POW[:, 0:8], -0.5)
            pool.memset(POW[:, 8:16], 0.5).then_inc(pool_consts, 1)
            pool.wait_ge(pool_consts, 2)
            pool.affine_select(out=IDENT[:], in_=IDENT[:], compare_op=ALU.not_equal, fill=1.0, base=0,
                               pattern=[[-1, P]], channel_multiplier=1).then_inc(pool_consts, 1)
            pool.wait_ge(pool_consts, 3)
            pool.tensor_copy(SEL[:], IDENT[0:E, 0:E].unsqueeze(2).to_broadcast([E, E, F])).then_inc(pool_consts, 1)

            def iteration(k, has):
                for u, j in ((1, k - 2), (0, k)):
                    if has[2 if u else 0]:
                        pool.wait_ge(gd[u], j * GD + 3)
                        pool.tensor_tensor(rstd[u][:], ve[u][:], POW[:, 0:1], ALU.pow).then_inc(gp[u], 1)
                if has[0]:
                    pool.wait_ge(pd, k * PD + 3)
                    pool.tensor_tensor(rstd[2][:], ve[2][:], POW[:, 0:1], ALU.pow).then_inc(pp, 1)
                    pool.wait_ge(pd, k * PD + 5)
                    pool.tensor_tensor(KSS[:, 1, :], KSS[:, 0, :], POW[:, 8:16], ALU.pow).then_inc(pp, 1)

            each_iteration(pool, iteration)

        @block.tensor
        def _(pe):
            pe.wait_ge(weights_in, 16 * 13)
            pe.wait_ge(pool_consts, 4)
            pe.wait_ge(dve_consts, 2)

            def gate_step(u, j, n):
                if n == 1:
                    pe.wait_ge(gd[u], j * GD + 4)
                    pe.transpose(gate_ps[u][:, 0:P], xn[u][:], IDENT[:]).then_inc(gt[u], 1)
                elif n == 2:
                    pe.wait_ge(ga[u], j * GA + 1)
                    pe.matmul(gate_ps[u][:, P:P + E], XT[:, u, :], CENT[:], start=True, stop=True).then_inc(gt[u], 1)
                elif n == 3:
                    pe.wait_ge(gd[u], j * GD + 13)
                    pe.transpose(gate_ps[u][:, 0:P], cw[u][:], IDENT[:]).then_inc(gt[u], 1)

            def up(k, e):
                if e >= 2:
                    pe.wait_ge(silu_done, k * CH + e - 1)
                    pe.wait_ge(gated, k * EC + e - 1)
                if e < EC:
                    pe.matmul(up_ps[e % 2][:, 0:256], WU[:, e, :, :], XT[:, :, :], start=True, stop=True)
                    pe.matmul(up_ps[e % 2][:, 256:512], SEL[:, 2 * e:2 * e + 2, :],
                              CT[:, :, :], start=True, stop=True).then_inc(up_done, 1)
                else:
                    pe.matmul(up_ps[e % 2][0:F, 0:256], WSU[:], XT[:, :, :], start=True, stop=True).then_inc(up_done, 1)

            def down(k, e):
                if e < EC:
                    pe.wait_ge(gated, k * EC + e + 1)
                    for u in range(2):
                        ins = pe.matmul(acc[u][:, 0:D], HG[:, e % 2, u, :], WD[:, e, :], start=(e == 0), stop=False)
                else:
                    pe.wait_ge(silu_done, k * CH + e + 1)
                    for u in range(2):
                        ins = pe.matmul(acc[u][:, 0:D], HSH[:, u, :], WSD[:], start=False, stop=True)
                ins.then_inc(down_done, 1)

            def cell_inputs(k, n):
                if n == 1:
                    pe.wait_ge(pd, k * PD + 4)
                    pe.transpose(cell_ps[:, 384:512], xn[2][:], IDENT[:]).then_inc(pt, 1)
                elif n == 2:
                    pe.wait_ge(pa, k * PA + 1)
                    pe.matmul(gate_ps[0][:, 384:512], WIN[:], XNT[:], start=True, stop=True).then_inc(pt, 1)
                elif n == 3:
                    pe.wait_ge(pa, k * PA + 2)
                    pe.matmul(kq_ps[:, 0:M], XP[:], WK[:], start=True, stop=True)
                    pe.matmul(kq_ps[:, M:2 * M], XP[:], WQ[:], start=True, stop=True)
                    for h in range(2):
                        pe.matmul(vb_ps[:, P * h:P * h + P], WV[:, P * h:P * h + P], XP[:], start=True, stop=True)
                        ins = pe.matmul(vb_ps[:, M + P * h:M + P * h + P], WB[:, P * h:P * h + P], XP[:], start=True, stop=True)
                    ins.then_inc(pt, 1)

            def row_sums(j, half):
                pe.wait_ge(pq_done, j * STEPS + HALF * (half + 1))
                for c in range(N):
                    ins = pe.matmul(cell_ps[:, P * half:P * half + P],
                                    IDENT[:], PQ[:, HALF * half:HALF * half + HALF, :, c],
                                    start=(c == 0), stop=(c == N - 1))
                ins.then_inc(sq_done, 1)

            def cell_output(j):
                pe.wait_ge(co_done, j + 1)
                for h in range(2):
                    ins = pe.matmul(cell_ps[:, 256:384], CO[:, h, :, :], WO[:, h, :],
                                    start=(h == 0), stop=(h == 1))
                ins.then_inc(y_done, 1)

            def iteration(k, has):
                if has[2]:
                    cell_output(k - 2)
                for n in (1, 2, 3):
                    if has[2]:
                        gate_step(1, k - 2, n)
                    if has[0]:
                        gate_step(0, k, n)
                if has[2]:
                    pe.wait_ge(ga[1], (k - 2) * GA + 3)
                if has[0]:
                    pe.wait_ge(ga[0], k * GA + 3)
                up(k, 0)
                up(k, 1)
                for e in range(CH):
                    down(k, e)
                    if e + 2 < CH:
                        up(k, e + 2)
                if has[0]:
                    for n in (1, 2, 3):
                        cell_inputs(k, n)
                if has[1]:
                    row_sums(k - 1, 0)
                    row_sums(k - 1, 1)

            each_iteration(pe, iteration)

        @block.scalar
        def _(act):
            act.preload_act_table_set("silu_and_others")
            act.wait_ge(weights_in, 16 * 13)
            act.wait_ge(dve_consts, 2)

            def gate_step(u, j, n):
                if n == 1:
                    act.wait_ge(gt[u], j * GT + 1)
                    act.copy(XT[:, u, :], gate_ps[u][:, 0:P]).then_inc(ga[u], 1)
                elif n == 2:
                    act.wait_ge(gt[u], j * GT + 2)
                    act.activation(th_aff[u][:], gate_ps[u][:, P:P + E], ACT.Tanh, scale=0.5).then_inc(ga[u], 1)
                elif n == 3:
                    act.wait_ge(gt[u], j * GT + 3)
                    act.copy(CT[:, u, :], gate_ps[u][0:E, 0:P]).then_inc(ga[u], 1)

            def silu(k, e):
                act.wait_ge(up_done, k * CH + e + 1)
                if e < EC:
                    if e >= 2:
                        act.wait_ge(gated, k * EC + e - 1)
                    act.activation(HS[:, e % 2, :, :], up_ps[e % 2][:, 0:256], ACT.Silu).then_inc(silu_done, 1)
                else:
                    act.activation(HSH[:], up_ps[e % 2][0:F, 0:256], ACT.Silu).then_inc(silu_done, 1)

            def cell_inputs(k, n):
                if n == 1:
                    act.wait_ge(pt, k * PT + 1)
                    act.copy(XNT[:], cell_ps[:, 384:512]).then_inc(pa, 1)
                elif n == 2:
                    act.wait_ge(pt, k * PT + 2)
                    act.activation(XP[:], gate_ps[0][:, 384:512], ACT.Silu).then_inc(pa, 1)
                elif n == 3:
                    act.wait_ge(pt, k * PT + 3)
                    act.activation(KSQ[:], kq_ps[:, 0:M], ACT.Square).then_inc(pa, 1)
                elif n == 4:
                    if not isinstance(k, int) or k >= 1:
                        act.wait_ge(q_stored, 64 * k)
                    act.copy(QT[:], kq_ps[:, M:2 * M]).then_inc(pa, 1)
                elif n == 5:
                    if not isinstance(k, int) or k >= 1:
                        act.wait_ge(v_placed, NGRP * k)
                    act.copy(VN[:].rearrange("p h b t -> p (h b t)"), vb_ps[:, 0:M]).then_inc(pa, 1)
                elif n in (6, 7):
                    h = n - 6
                    if n == 6 and (not isinstance(k, int) or k >= 1):
                        act.wait_ge(beta_placed, k)
                    act.activation(BN[:, h, :, :].rearrange("p b t -> p (b t)"), vb_ps[:, M + P * h:M + P * h + P], ACT.Tanh,
                                   bias=HB[:, h:h + 1], scale=0.5).then_inc(pa, 1)

            HB = sb("HB", [P, 2])
            half_bias = sem("half_bias")
            act.mul(HB[:], BB[:], 0.5).then_inc(half_bias, 1)
            act.wait_ge(half_bias, 1)

            def decayed(j, t, h):
                act.wait_ge(s_done, j * 2 * STEPS + 2 * t + h + 1)
                for hh in range(2):
                    g = 2 * h + hh
                    ins = act.activation(QS[:, g, :], SR[:, (t - 1) % RING, g, 0:N], ACT.Identity,
                                         scale=BT[:, hh, h, t:t + 1])
                ins.then_inc(bs_done, 1)

            def new_state(j, t, h):
                act.wait_ge(u_done, j * 2 * STEPS + 2 * t + h + 1)
                act.activation(SR[:, t % RING, g_of(h), 0:N], UU[:, g_of(h), :], ACT.Tanh).then_inc(s_done, 1)

            def iteration(k, has):
                if has[2]:
                    act.wait_ge(sq_done, 2 * (k - 1))
                    act.activation(SQS[:].rearrange("p t g -> p (t g)"), cell_ps[:, 0:256], ACT.Silu).then_inc(osilu_done, 1)
                for n in (1, 2, 3):
                    if has[2]:
                        gate_step(1, k - 2, n)
                    if has[0]:
                        gate_step(0, k, n)
                for e in range(CH):
                    silu(k, e)
                if has[0]:
                    for n in range(1, PA + 1):
                        cell_inputs(k, n)
                if has[1]:
                    act.wait_ge(beta_placed, k)
                    for h in range(2):
                        decayed(k - 1, 0, h)
                    for t in range(STEPS):
                        for h in range(2):
                            new_state(k - 1, t, h)
                            if t + 1 < STEPS:
                                decayed(k - 1, t + 1, h)

            each_iteration(act, iteration)

        @block.vector
        def _(dve):
            dve.memset(SR[:], 0.0).then_inc(dve_consts, 1)
            dve.memset(KT[:, :, N:W1], 0.0)
            dve.memset(XT[:], 0.0)
            for u in range(2):
                dve.memset(cw[u][:, E:P], 0.0)
            dve.memset(CT[:], 0.0).then_inc(dve_consts, 1)
            dve.wait_ge(dve_consts, 1)
            dve.memset(SR[:, :, :, N:W1], 1.0).then_inc(s_done, 2)
            dve.wait_ge(weights_in, 16 * 13)

            def steady():
                dve.sem_inc(carried, 1)

            def normalise(u, src, n, done, per, j):
                if n == 1:
                    dve.bn_stats(st[u][:], src).then_inc(done, 1)
                elif n == 2:
                    dve.wait_ge(done, j * per + 1)
                    steady()
                    dve.bn_aggr(mv[u][:], st[u][:]).then_inc(done, 1)
                elif n == 3:
                    dve.wait_ge(done, j * per + 2)
                    dve.tensor_scalar(ve[u][:], mv[u][:, 1:2], LN_EPS, None, ALU.add).then_inc(done, 1)
                elif n == 4:
                    dve.tensor_scalar(xn[u][:], src, mv[u][:, 0:1], rstd[u][:], ALU.subtract, ALU.mult).then_inc(done, 1)

            def gate_step(u, j, n):
                src, done = (X2 if u else XA)[:], gd[u]
                if n == 1:
                    if u:
                        dve.wait_ge(x2_done, j + 1)
                    else:
                        dve.wait_ge(x_in, 32 * (j + 1))
                if n == 4:
                    dve.wait_ge(gp[u], j + 1)
                if n <= 4:
                    normalise(u, src, n, done, GD, j)
                elif n == 5:
                    dve.wait_ge(ga[u], j * GA + 2)
                    dve.tensor_tensor(biased[u][:], gate_ps[u][:, P:P + E], EB[:], ALU.add).then_inc(done, 1)
                elif n == 6:
                    dve.wait_ge(done, j * GD + 5)
                    steady()
                    dve.max(top8[u][:], biased[u][:]).then_inc(done, 1)
                elif n == 7:
                    dve.wait_ge(done, j * GD + 6)
                    steady()
                    dve.match_replace(rest[u][:], top8[u][:], biased[u][:], -3.0e38).then_inc(done, 1)
                elif n == 8:
                    dve.wait_ge(done, j * GD + 7)
                    dve.tensor_tensor(chosen[u][:], rest[u][:], biased[u][:], ALU.not_equal).then_inc(done, 1)
                elif n == 9:
                    dve.wait_ge(done, j * GD + 8)
                    dve.scalar_tensor_tensor(w2[u][:], th_aff[u][:], 1.0, chosen[u][:], ALU.add, ALU.mult).then_inc(done, 1)
                elif n == 10:
                    dve.wait_ge(done, j * GD + 9)
                    dve.tensor_reduce(wsum[u][:, 0:1], w2[u][:], AX.X, ALU.add).then_inc(done, 1)
                elif n == 11:
                    dve.wait_ge(done, j * GD + 10)
                    dve.tensor_scalar(wsum[u][:, 1:2], wsum[u][:, 0:1], 0.5, SUM_EPS, ALU.mult, ALU.add).then_inc(done, 1)
                elif n == 12:
                    dve.wait_ge(done, j * GD + 11)
                    dve.reciprocal(wsum[u][:, 2:3], wsum[u][:, 1:2]).then_inc(done, 1)
                elif n == 13:
                    dve.wait_ge(done, j * GD + 12)
                    dve.tensor_scalar(cw[u][:, 0:E], w2[u][:], wsum[u][:, 2:3], 0.5, ALU.mult, ALU.mult).then_inc(done, 1)

            def gate(k, e):
                dve.wait_ge(silu_done, k * CH + e + 1)
                if e >= 2:
                    dve.wait_ge(down_done, k * CH + e - 1)
                dve.tensor_tensor(HG[:, e % 2, :, :].rearrange("p u t -> p (u t)"), HS[:, e % 2, :, :].rearrange("p u t -> p (u t)"),
                                  up_ps[e % 2][:, 256:512], ALU.mult).then_inc(gated, 1)

            def ffn_sums(k, has):
                dve.wait_ge(down_done, (k + 1) * CH)
                if has[0]:
                    if not isinstance(k, int) or k >= 1:
                        dve.tensor_copy(X1P[:], X1N[:]).then_inc(x1_done, 1)
                    else:
                        dve.memset(X1P[:], 0.0).then_inc(x1_done, 1)
                    dve.wait_ge(x1_done, 2 * k + 1)
                    dve.scalar_tensor_tensor(X1N[:], acc[0][:, 0:D], 0.5, XA[:], ALU.mult, ALU.add).then_inc(x1_done, 1)
                if has[2]:
                    if not isinstance(k, int) or k > 2:
                        dve.wait_ge(out_stored, 32 * (k - 2))
                    dve.scalar_tensor_tensor(OT[:], acc[1][:, 0:D], 0.5, X2[:], ALU.mult, ALU.add).then_inc(out_ready, 1)

            def cell_inputs(k, n):
                if n == 1:
                    dve.wait_ge(x1_done, 2 * k + 2)
                if n == 4:
                    dve.wait_ge(pp, k * PP + 1)
                if n <= 4:
                    normalise(2, X1N[:], n, pd, PD, k)
                elif n == 5:
                    dve.wait_ge(pa, k * PA + 3)
                    dve.tensor_reduce(KSS[:, 0, :], KSQ[:].rearrange("p (h n) -> p h n", h=HEADS), AX.X, ALU.add).then_inc(pd, 1)
                elif n == 6:
                    dve.wait_ge(pp, k * PP + 2)
                    dve.tensor_scalar(KSS[:, 2, :], KSS[:, 1, :], NORM_EPS, -1.0, ALU.add, ALU.mult).then_inc(pd, 1)
                elif n == 7:
                    dve.wait_ge(pd, k * PD + 6)
                    dve.reciprocal(KSS[:, 3, :], KSS[:, 2, :]).then_inc(pd, 1)
                elif n == 8:
                    if not isinstance(k, int) or k >= 1:
                        dve.wait_ge(k_stored, 64 * k)
                    dve.wait_ge(pa, k * PA + 4)
                    dve.wait_ge(pd, k * PD + 7)
                    dve.tensor_tensor(KT[:, :, 0:N], kq_ps[:, 0:M].rearrange("p (h n) -> p h n", h=HEADS),
                                      KSS[:, 3, :].unsqueeze(2).to_broadcast([P, HEADS, N]), ALU.mult).then_inc(pd, 1)
                elif n == 9:
                    dve.wait_ge(pa, k * PA + 7)
                    dve.tensor_scalar(BN[:], BN[:], 0.5, 0.5, ALU.mult, ALU.add).then_inc(pd, 1)

            def place(k):
                dve.wait_ge(pd, k * PD + 9)
                dve.tensor_copy(BT[:], BN[:]).then_inc(beta_placed, 1)
                for r in range(NGRP):
                    dve.wait_ge(kb_in[r], 64 * (k + 1))
                    for b in range(B):
                        steps = slice(GRP * r, GRP * r + GRP)
                        ins = dve.tensor_copy(KB[:, steps, 2 * b:2 * b + 2, N], VN[:, :, b, steps].rearrange("p h t -> p t h"))
                    ins.then_inc(v_placed, 1)

            def n_of(j, t, h):
                return j * 2 * STEPS + 2 * t + h + 1

            def prod(j, t, h):
                if h == 0 and t % GRP == 0:
                    dve.wait_ge(v_placed, NGRP * j + t // GRP + 1)
                dve.wait_ge(s_done, n_of(j, t, h))
                dve.tensor_tensor(PR[:, g_of(h), :], SR[:, (t - 1) % RING, g_of(h), :], KB[:, t, g_of(h), :],
                                  ALU.mult).then_inc(prod_done, 1)

            def delta(j, t, h):
                dve.wait_ge(prod_done, n_of(j, t, h))
                dve.tensor_reduce(DEL[:, g_of(h)], PR[:, g_of(h), :], AX.X, ALU.add).then_inc(delta_done, 1)

            def outer(j, t, h):
                dve.wait_ge(delta_done, n_of(j, t, h))
                dve.tensor_tensor(WT[:, g_of(h), :], KB[:, t, g_of(h), 0:N],
                                  DEL[:, g_of(h)].unsqueeze(2).to_broadcast([P, 2, N]), ALU.mult).then_inc(outer_done, 1)

            def add(j, t, h):
                dve.wait_ge(outer_done, n_of(j, t, h))
                dve.wait_ge(bs_done, n_of(j, t, h))
                dve.tensor_tensor(UU[:, g_of(h), :], QS[:, g_of(h), :], WT[:, g_of(h), :], ALU.subtract).then_inc(u_done, 1)

            def times_q(j, t):
                if t % GRP == 0:
                    dve.wait_ge(qb_in[t // GRP], 64 * (j + 1))
                if t % HALF == 0 and (not isinstance(j, int) or j >= 1):
                    dve.wait_ge(sq_done, 2 * (j - 1) + t // HALF + 1)
                dve.wait_ge(s_done, n_of(j, t, 1) + 2)
                dve.tensor_tensor(PQ[:, t, :, :], SR[:, t % RING, :, 0:N], QB[:, t, :, :], ALU.mult).then_inc(pq_done, 1)

            def iteration(k, has):
                if has[2]:
                    j = k - 2
                    dve.wait_ge(osilu_done, j + 1)
                    dve.tensor_tensor(CO[:].rearrange("p h b t -> p t b h"), SQS[:].rearrange("p t (b h) -> p t b h", b=B),
                                      cell_ps[:, 0:256].rearrange("p (t b h) -> p t b h", b=B, h=2), ALU.mult).then_inc(co_done, 1)
                    dve.wait_ge(y_done, j + 1)
                    x1 = X1N if isinstance(k, int) and k > TILES else X1P
                    dve.tensor_tensor(X2[:], cell_ps[:, 256:384], x1[:], ALU.add).then_inc(x2_done, 1)
                for n in range(1, GD + 1):
                    if has[2]:
                        gate_step(1, k - 2, n)
                    if has[0]:
                        gate_step(0, k, n)
                for e in range(EC):
                    gate(k, e)
                ffn_sums(k, has)
                if has[0]:
                    for n in range(1, PD + 1):
                        cell_inputs(k, n)
                if has[1]:
                    j = k - 1
                    for t in range(STEPS):
                        prod(j, t, 0)
                        if t:
                            add(j, t - 1, 1)
                        delta(j, t, 0)
                        outer(j, t, 0)
                        if t:
                            times_q(j, t - 1)
                        prod(j, t, 1)
                        add(j, t, 0)
                        delta(j, t, 1)
                        outer(j, t, 1)
                    add(j, STEPS - 1, 1)
                    times_q(j, STEPS - 1)
                if has[0]:
                    place(k)

            each_iteration(dve, iteration)


def kernel(L0_attn_x, L0_attn_W_in, L0_attn_W_k, L0_attn_W_v, L0_attn_W_q, L0_attn_W_beta, L0_attn_b_beta, L0_attn_W_out,
           L0_ffn_centroids, L0_ffn_expert_biases, L0_ffn_Ws_up, L0_ffn_Ws_down, L0_ffn_W_up, L0_ffn_W_down):
    import numpy as np
    import concourse.bacc as bacc
    from concourse.bass_utils import run_bass_kernel_spmd

    nc = bacc.Bacc("TRN2", target_bir_lowering=False, num_devices=1)
    laid_out = {
        "x": L0_attn_x, "w_in": L0_attn_W_in.T, "w_k": L0_attn_W_k.T, "w_v": L0_attn_W_v.T, "w_q": L0_attn_W_q.T,
        "w_beta": L0_attn_W_beta.T, "b_beta": L0_attn_b_beta.reshape(2, P).T, "w_out": L0_attn_W_out.T, "cent": L0_ffn_centroids.T,
        "ebias": L0_ffn_expert_biases, "ws_up": L0_ffn_Ws_up, "ws_down": L0_ffn_Ws_down, "w_up": L0_ffn_W_up,
        "w_down": L0_ffn_W_down,
    }
    arrays, args = {}, []
    for name, a in laid_out.items():
        a = np.ascontiguousarray(a)
        arrays[f"in_{name}"] = a
        args.append(nc.dram_tensor(f"in_{name}", a.shape, F32, kind="ExternalInput").ap())
    args.append(nc.dram_tensor("out_y", (B, T, D), F32, kind="ExternalOutput").ap())
    args.append(nc.dram_tensor("key_rows", (4, STEPS, G, W1), F32, kind="Internal").ap())
    args.append(nc.dram_tensor("query_rows", (4, STEPS, G, N), F32, kind="Internal").ap())
    macaron_program(nc, *args)
    r = run_bass_kernel_spmd(nc, [arrays], core_ids=[0])
    return r.results[0]["out_y"]
```

```python
from contextlib import ExitStack

import concourse.bass as bass
from concourse import mybir

F32 = mybir.dt.float32
ALU = mybir.AluOpType
ACT = mybir.ActivationFunctionType
AX = mybir.AxisListType

P = 128
D = 128
HEADS, N = 8, 32
M = HEADS * N
E, F = 64, 64
EC = E * F // P
B, T = 2, 1024
STEPS = 64
TILES = T // STEPS
G = 4
GRP = 16
NGRP = STEPS // GRP
RING = 32
HALF = STEPS // 2
W1 = N + 1
LN_EPS, NORM_EPS, SUM_EPS = 1e-5, 1e-6, 1e-8
DEEP = 4
CH = EC + 1

SLOTS = 2 * STEPS
GATE_AT = (8, 19)
GATE_DVE = (0, 1, 2, 4, 9, 10, 11, 12, 13, 14, 15, 16, 17)
GATE_ACT = (6, 8, 19)
CELL_OUT_ACT, CELL_OUT_DVE = 12, (13, 17)
FFN_AT, FFN_SPAN = 38, 52
SUMS_AT = FFN_AT + FFN_SPAN + 4
INPUTS_AT = SUMS_AT + 1
INPUTS_DVE = (0, 1, 2, 4, 10, 12, 13, 14, 15)
INPUTS_ACT = (5, 7, 9, 10, 11, 12, 13)


def ffn_slot(e):
    return FFN_AT + e * FFN_SPAN // EC


GD, GT, GA = 13, 3, 3
PD, PP, PT, PA = 9, 2, 3, 7
BCAST = 0


def macaron_program(nc, x, w_in, w_k, w_v, w_q, w_beta, b_beta, w_out, cent, ebias, ws_up, ws_down, w_up, w_down,
                    out, key_rows, query_rows):
    with ExitStack() as ctx:
        def sb(name, shape):
            return ctx.enter_context(nc.sbuf_tensor(name, shape, F32))

        def ps(name):
            return ctx.enter_context(nc.psum_tensor(name, [P, 512], F32))

        def sem(name):
            return ctx.enter_context(nc.semaphore(name))

        WU = sb("WU", [P, EC, 2, F])
        WD = sb("WD", [P, EC, D])
        WSU = sb("WSU", [P, F])
        WSD = sb("WSD", [F, D])
        CENT = sb("CENT", [P, E])
        EB = sb("EB", [P, E])
        WIN = sb("WIN", [P, D])
        WK = sb("WK", [P, M])
        WQ = sb("WQ", [P, M])
        WV = sb("WV", [P, M])
        WB = sb("WB", [P, M])
        WO = sb("WO", [P, 2, D])
        BB = sb("BB", [P, 2])
        IDENT = sb("IDENT", [P, P])
        SEL = sb("SEL", [E, E, F])
        POW = sb("POW", [P, 16])
        XA = sb("XA", [P, D])
        X1N = sb("X1N", [P, D])
        X1P = sb("X1P", [P, D])
        X2 = sb("X2", [P, D])
        OT = sb("OT", [P, D])
        XT = sb("XT", [P, 2, P])
        CT = sb("CT", [E, 2, P])
        HS = sb("HS", [P, DEEP, 2, P])
        HG = sb("HG", [P, DEEP, 2, P])
        HSH = sb("HSH", [F, 2, P])
        st = [sb(f"st{u}", [P, 6]) for u in range(3)]
        mv = [sb(f"mv{u}", [P, 2]) for u in range(3)]
        ve = [sb(f"ve{u}", [P, 1]) for u in range(3)]
        rstd = [sb(f"rstd{u}", [P, 1]) for u in range(3)]
        xn = [sb(f"xn{u}", [P, D]) for u in range(3)]
        biased = [sb(f"biased{u}", [P, E]) for u in range(2)]
        top8 = [sb(f"top8{u}", [P, 8]) for u in range(2)]
        rest = [sb(f"rest{u}", [P, E]) for u in range(2)]
        chosen = [sb(f"chosen{u}", [P, E]) for u in range(2)]
        th_aff = [sb(f"th_aff{u}", [P, E]) for u in range(2)]
        w2 = [sb(f"w2{u}", [P, E]) for u in range(2)]
        wsum = [sb(f"wsum{u}", [P, 3]) for u in range(2)]
        cw = [sb(f"cw{u}", [P, P]) for u in range(2)]
        XNT = sb("XNT", [P, P])
        XP = sb("XP", [P, P])
        KSQ = sb("KSQ", [P, M])
        KSS = sb("KSS", [P, 4, HEADS])
        KT = sb("KT", [P, HEADS, W1])
        QT = sb("QT", [P, M])
        VN = sb("VN", [P, 2, B, STEPS])
        BN = sb("BN", [P, 2, B, STEPS])
        BT = sb("BT", [P, 2, B, STEPS])
        KB = sb("KB", [P, STEPS, G, W1])
        QB = sb("QB", [P, STEPS, G, N])
        SR = sb("SR", [P, RING, G, W1])
        PR = sb("PR", [P, G, W1])
        DEL = sb("DEL", [P, G])
        WT = sb("WT", [P, G, N])
        QS = sb("QS", [P, G, N])
        UU = sb("UU", [P, G, N])
        PQ = sb("PQ", [P, STEPS, G, N])
        SQS = sb("SQS", [P, STEPS, G])
        CO = sb("CO", [P, 2, B, STEPS])

        acc = [ps("acc0"), ps("acc1")]
        cell_ps = ps("cell_ps")
        kq_ps = ps("kq_ps")
        vb_ps = ps("vb_ps")
        up_ps = [ps("up0"), ps("up1"), kq_ps, vb_ps]
        gate_ps = [ps("gate_ps"), vb_ps]

        weights_in = sem("weights_in")
        pool_consts, dve_consts = sem("pool_consts"), sem("dve_consts")
        x_in = sem("x_in")
        gd = [sem("gd0"), sem("gd1")]
        gp = [sem("gp0"), sem("gp1")]
        gt = [sem("gt0"), sem("gt1")]
        ga = [sem("ga0"), sem("ga1")]
        up_done, silu_done, gated, down_done = sem("up_done"), sem("silu_done"), sem("gated"), sem("down_done")
        x1_done, out_ready, out_stored = sem("x1_done"), sem("out_ready"), sem("out_stored")
        pd, pp, pt, pa = sem("pd"), sem("pp"), sem("pt"), sem("pa")
        k_stored, q_stored, v_placed, beta_placed = (sem(s) for s in ("k_stored", "q_stored", "v_placed", "beta_placed"))
        kb_in = [sem(f"kb_in{r}") for r in range(NGRP)]
        qb_in = [sem(f"qb_in{r}") for r in range(NGRP)]
        prod_done, delta_done, outer_done, u_done, s_done, bs_done, pq_done = (sem(s) for s in (
            "prod_done", "delta_done", "outer_done", "u_done", "s_done", "bs_done", "pq_done"))
        sq_done, osilu_done, co_done, y_done, x2_done = (sem(s) for s in (
            "sq_done", "osilu_done", "co_done", "y_done", "x2_done"))

        carried = sem("carried")

        def each_iteration(eng, body):
            body(0, (True, False, False))
            body(1, (True, True, False))
            with eng.Fori(2, TILES - 1) as k:
                body(k, (True, True, True))
            body(TILES - 1, (True, True, True))
            body(TILES, (False, True, True))
            body(TILES + 1, (False, False, True))

        def g_of(h):
            return slice(2 * h, 2 * h + 2)

        NW = 15
        block = ctx.enter_context(nc.Block())

        @block.sync
        def _(sp):
            sp.dma_start(XA[0:STEPS, :], x[0, 0:STEPS, :]).then_inc(x_in, 16)
            sp.dma_start(XA[STEPS:P, :], x[1, 0:STEPS, :]).then_inc(x_in, 16)
            for dst, src in ((CENT[:], cent), (EB[:], ebias.partition_broadcast(P)), (WSU[:], ws_up), (WSD[:], ws_down),
                             (WU[:], w_up.rearrange("(c m) d f -> d c m f", m=2)),
                             (WD[:], w_down.rearrange("(c m) f d -> (m f) c d", m=2)),
                             (WIN[:], w_in), (WK[:], w_k), (WQ[:], w_q), (WV[:], w_v), (WB[:], w_beta),
                             (WO[:], w_out.rearrange("(h p) d -> p h d", h=2)),
                             (BB[:], b_beta)):
                sp.dma_start(dst, src).then_inc(weights_in, 16)

            def iteration(k, has):
                if has[0]:
                    for b in range(B):
                        if b == 0:
                            sp.wait_ge(pd, k * PD + 8)
                        dst = key_rows.rearrange("s t (b h) w -> b t h s w", b=B)[b]
                        for h in range(2):
                            sp.dma_start(dst[:, h], KT[b * STEPS:(b + 1) * STEPS, 4 * h:4 * h + 4, :]).then_inc(k_stored, 16)
                    for b in range(B):
                        if b == 0:
                            sp.wait_ge(pa, k * PA + 4)
                        dst = query_rows.rearrange("s t (b h) w -> b t h s w", b=B)[b]
                        for h in range(2):
                            sp.dma_start(dst[:, h], QT[b * STEPS:(b + 1) * STEPS, 128 * h:128 * h + 128].rearrange(
                                "t (s w) -> t s w", s=4)).then_inc(q_stored, 16)
                    sp.wait_ge(x1_done, 2 * k + 2)
                    sp.sem_inc(carried, 1)
                    if not isinstance(k, int) or k + 1 < TILES:
                        for b in range(B):
                            sp.dma_start(XA[b * STEPS:(b + 1) * STEPS, :],
                                         x[b, bass.ds((k + 1) * STEPS, STEPS), :]).then_inc(x_in, 16)
                if has[2]:
                    sp.wait_ge(out_ready, k - 1)
                    sp.sem_inc(carried, 1)
                    for b in range(B):
                        sp.dma_start(out[b, bass.ds((k - 2) * STEPS, STEPS), :],
                                     OT[b * STEPS:(b + 1) * STEPS, :]).then_inc(out_stored, 16)
                if has[0]:
                    sp.wait_ge(k_stored, 64 * (k + 1))
                    sp.wait_ge(q_stored, 64 * (k + 1))
                    for r in range(NGRP):
                        if has[1]:
                            sp.wait_ge(pq_done, (k - 1) * STEPS + GRP * (r + 1))
                        for s in range(4):
                            rows = slice(N * s, N * s + N)
                            steps = slice(GRP * r, GRP * r + GRP)
                            sp.dma_start(KB[rows, steps, :, :].rearrange("p t g w -> p (t g w)"),
                                         key_rows[s, steps].rearrange("t g w -> (t g w)").partition_broadcast(N)).then_inc(kb_in[r], 16)
                            sp.dma_start(QB[rows, steps, :, :].rearrange("p t g w -> p (t g w)"),
                                         query_rows[s, steps].rearrange("t g w -> (t g w)").partition_broadcast(N)).then_inc(qb_in[r], 16)
                    for r in range(NGRP):
                        sp.wait_ge(kb_in[r], 64 * (k + 1))
                        sp.wait_ge(qb_in[r], 64 * (k + 1))
                    sp.sem_inc(carried, 1)

            each_iteration(sp, iteration)
            sp.wait_ge(out_stored, 32 * TILES)

        @block.gpsimd
        def _(pool):
            pool.memset(IDENT[:], 0.0).then_inc(pool_consts, 1)
            pool.memset(POW[:, 0:8], -0.5)
            pool.memset(POW[:, 8:16], 0.5).then_inc(pool_consts, 1)
            pool.wait_ge(pool_consts, 2)
            pool.affine_select(out=IDENT[:], in_=IDENT[:], compare_op=ALU.not_equal, fill=1.0, base=0,
                               pattern=[[-1, P]], channel_multiplier=1).then_inc(pool_consts, 1)
            pool.wait_ge(pool_consts, 3)
            pool.tensor_copy(SEL[:], IDENT[0:E, 0:E].unsqueeze(2).to_broadcast([E, E, F])).then_inc(pool_consts, 1)

            def iteration(k, has):
                for u, j in ((0, k), (1, k - 2)):
                    if has[2 if u else 0]:
                        pool.wait_ge(gd[u], j * GD + 3)
                        pool.tensor_tensor(rstd[u][:], ve[u][:], POW[:, 0:1], ALU.pow).then_inc(gp[u], 1)
                if has[0]:
                    pool.wait_ge(pd, k * PD + 3)
                    pool.tensor_tensor(rstd[2][:], ve[2][:], POW[:, 0:1], ALU.pow).then_inc(pp, 1)
                    pool.wait_ge(pd, k * PD + 5)
                    pool.tensor_tensor(KSS[:, 1, :], KSS[:, 0, :], POW[:, 8:16], ALU.pow).then_inc(pp, 1)

            each_iteration(pool, iteration)

        @block.tensor
        def _(pe):
            pe.wait_ge(weights_in, 16 * 13)
            pe.wait_ge(pool_consts, 4)
            pe.wait_ge(dve_consts, 2)

            def gate_step(u, j, n):
                if n == 1:
                    pe.wait_ge(gd[u], j * GD + 4)
                    pe.transpose(gate_ps[u][:, 0:P], xn[u][:], IDENT[:]).then_inc(gt[u], 1)
                elif n == 2:
                    pe.wait_ge(ga[u], j * GA + 1)
                    pe.matmul(gate_ps[u][:, P:P + E], XT[:, u, :], CENT[:], start=True, stop=True).then_inc(gt[u], 1)
                elif n == 3:
                    pe.wait_ge(gd[u], j * GD + 13)
                    pe.transpose(gate_ps[u][:, 0:P], cw[u][:], IDENT[:]).then_inc(gt[u], 1)

            def up(k, e):
                if e >= DEEP:
                    pe.wait_ge(silu_done, k * CH + e - DEEP + 1)
                    pe.wait_ge(gated, k * EC + e - DEEP + 1)
                if e < EC:
                    pe.matmul(up_ps[e % DEEP][:, 0:256], WU[:, e, :, :], XT[:, :, :], start=True, stop=True)
                    pe.matmul(up_ps[e % DEEP][:, 256:512], SEL[:, 2 * e:2 * e + 2, :],
                              CT[:, :, :], start=True, stop=True).then_inc(up_done, 1)
                else:
                    pe.matmul(up_ps[e % DEEP][0:F, 0:256], WSU[:], XT[:, :, :], start=True, stop=True).then_inc(up_done, 1)

            def down(k, e):
                if e < EC:
                    pe.wait_ge(gated, k * EC + e + 1)
                    for u in range(2):
                        ins = pe.matmul(acc[u][:, 0:D], HG[:, e % DEEP, u, :], WD[:, e, :], start=(e == 0), stop=False)
                else:
                    pe.wait_ge(silu_done, k * CH + e + 1)
                    for u in range(2):
                        ins = pe.matmul(acc[u][:, 0:D], HSH[:, u, :], WSD[:], start=False, stop=True)
                ins.then_inc(down_done, 1)

            def cell_inputs(k, n):
                if n == 1:
                    pe.wait_ge(pd, k * PD + 4)
                    pe.transpose(cell_ps[:, 384:512], xn[2][:], IDENT[:]).then_inc(pt, 1)
                elif n == 2:
                    pe.wait_ge(pa, k * PA + 1)
                    pe.matmul(gate_ps[0][:, 384:512], WIN[:], XNT[:], start=True, stop=True).then_inc(pt, 1)
                elif n == 3:
                    pe.wait_ge(pa, k * PA + 2)
                    pe.matmul(kq_ps[:, 0:M], XP[:], WK[:], start=True, stop=True)
                    pe.matmul(kq_ps[:, M:2 * M], XP[:], WQ[:], start=True, stop=True)
                    for h in range(2):
                        pe.matmul(vb_ps[:, P * h:P * h + P], WV[:, P * h:P * h + P], XP[:], start=True, stop=True)
                        ins = pe.matmul(vb_ps[:, M + P * h:M + P * h + P], WB[:, P * h:P * h + P], XP[:], start=True, stop=True)
                    ins.then_inc(pt, 1)

            def row_sums(j, half):
                pe.wait_ge(pq_done, j * STEPS + HALF * (half + 1))
                for c in range(N):
                    ins = pe.matmul(cell_ps[:, P * half:P * half + P],
                                    IDENT[:], PQ[:, HALF * half:HALF * half + HALF, :, c],
                                    start=(c == 0), stop=(c == N - 1))
                ins.then_inc(sq_done, 1)

            def cell_output(j):
                pe.wait_ge(co_done, j + 1)
                for h in range(2):
                    ins = pe.matmul(cell_ps[:, 256:384], CO[:, h, :, :], WO[:, h, :],
                                    start=(h == 0), stop=(h == 1))
                ins.then_inc(y_done, 1)

            def iteration(k, has):
                if has[2]:
                    row_sums(k - 2, 1)
                if has[0]:
                    gate_step(0, k, 1)
                    gate_step(0, k, 2)
                if has[2]:
                    cell_output(k - 2)
                if has[0]:
                    gate_step(0, k, 3)
                if has[2]:
                    for n in (1, 2, 3):
                        gate_step(1, k - 2, n)
                if has[2]:
                    pe.wait_ge(ga[1], (k - 2) * GA + 3)
                if has[0]:
                    pe.wait_ge(ga[0], k * GA + 3)
                for e in range(DEEP):
                    up(k, e)
                for e in range(CH):
                    down(k, e)
                    if e + DEEP < CH:
                        up(k, e + DEEP)
                if has[0]:
                    for n in (1, 2, 3):
                        cell_inputs(k, n)
                if has[1]:
                    row_sums(k - 1, 0)

            each_iteration(pe, iteration)

        @block.scalar
        def _(act):
            act.preload_act_table_set("silu_and_others")
            act.wait_ge(weights_in, 16 * 13)
            act.wait_ge(dve_consts, 2)

            def gate_step(u, j, n):
                if n == 1:
                    act.wait_ge(gt[u], j * GT + 1)
                    act.copy(XT[:, u, :], gate_ps[u][:, 0:P]).then_inc(ga[u], 1)
                elif n == 2:
                    act.wait_ge(gt[u], j * GT + 2)
                    act.activation(th_aff[u][:], gate_ps[u][:, P:P + E], ACT.Tanh, scale=0.5).then_inc(ga[u], 1)
                elif n == 3:
                    act.wait_ge(gt[u], j * GT + 3)
                    act.copy(CT[:, u, :], gate_ps[u][0:E, 0:P]).then_inc(ga[u], 1)

            def silu(k, e):
                act.wait_ge(up_done, k * CH + e + 1)
                if e < EC:
                    if e >= DEEP:
                        act.wait_ge(gated, k * EC + e - DEEP + 1)
                    act.activation(HS[:, e % DEEP, :, :], up_ps[e % DEEP][:, 0:256], ACT.Silu).then_inc(silu_done, 1)
                else:
                    act.activation(HSH[:], up_ps[e % DEEP][0:F, 0:256], ACT.Silu).then_inc(silu_done, 1)

            def cell_inputs(k, n):
                if n == 1:
                    act.wait_ge(pt, k * PT + 1)
                    act.copy(XNT[:], cell_ps[:, 384:512]).then_inc(pa, 1)
                elif n == 2:
                    act.wait_ge(pt, k * PT + 2)
                    act.activation(XP[:], gate_ps[0][:, 384:512], ACT.Silu).then_inc(pa, 1)
                elif n == 3:
                    act.wait_ge(pt, k * PT + 3)
                    act.activation(KSQ[:], kq_ps[:, 0:M], ACT.Square).then_inc(pa, 1)
                elif n == 4:
                    if not isinstance(k, int) or k >= 1:
                        act.wait_ge(q_stored, 64 * k)
                    act.copy(QT[:], kq_ps[:, M:2 * M]).then_inc(pa, 1)
                elif n == 5:
                    if not isinstance(k, int) or k >= 1:
                        act.wait_ge(v_placed, NGRP * k)
                    act.copy(VN[:].rearrange("p h b t -> p (h b t)"), vb_ps[:, 0:M]).then_inc(pa, 1)
                elif n in (6, 7):
                    h = n - 6
                    if n == 6 and (not isinstance(k, int) or k >= 1):
                        act.wait_ge(beta_placed, k)
                    act.activation(BN[:, h, :, :].rearrange("p b t -> p (b t)"), vb_ps[:, M + P * h:M + P * h + P], ACT.Tanh,
                                   bias=HB[:, h:h + 1], scale=0.5).then_inc(pa, 1)

            HB = sb("HB", [P, 2])
            half_bias = sem("half_bias")
            act.mul(HB[:], BB[:], 0.5).then_inc(half_bias, 1)
            act.wait_ge(half_bias, 1)

            def decayed(j, t, h):
                act.wait_ge(s_done, j * 2 * STEPS + 2 * t + h + 1)
                for hh in range(2):
                    g = 2 * h + hh
                    ins = act.activation(QS[:, g, :], SR[:, (t - 1) % RING, g, 0:N], ACT.Identity,
                                         scale=BT[:, hh, h, t:t + 1])
                ins.then_inc(bs_done, 1)

            def new_state(j, t, h):
                act.wait_ge(u_done, j * 2 * STEPS + 2 * t + h + 1)
                act.activation(SR[:, t % RING, g_of(h), 0:N], UU[:, g_of(h), :], ACT.Tanh).then_inc(s_done, 1)

            def background(k, has, slot):
                if has[2] and slot == CELL_OUT_ACT:
                    act.wait_ge(sq_done, 2 * (k - 1))
                    act.activation(SQS[:].rearrange("p t g -> p (t g)"), cell_ps[:, 0:256], ACT.Silu).then_inc(osilu_done, 1)
                for n in range(GA):
                    if has[0] and slot == GATE_AT[0] + GATE_ACT[n]:
                        gate_step(0, k, n + 1)
                    if has[2] and slot == GATE_AT[1] + GATE_ACT[n]:
                        gate_step(1, k - 2, n + 1)
                for e in range(CH):
                    if slot == ffn_slot(e):
                        silu(k, e)
                for n in range(PA):
                    if has[0] and slot == INPUTS_AT + INPUTS_ACT[n]:
                        cell_inputs(k, n + 1)

            def iteration(k, has):
                if has[1]:
                    act.wait_ge(beta_placed, k)
                    for h in range(2):
                        decayed(k - 1, 0, h)
                for t in range(STEPS):
                    for h in range(2):
                        if has[1]:
                            new_state(k - 1, t, h)
                            if t + 1 < STEPS:
                                decayed(k - 1, t + 1, h)
                        background(k, has, 2 * t + h)

            each_iteration(act, iteration)

        @block.vector
        def _(dve):
            dve.memset(SR[:], 0.0).then_inc(dve_consts, 1)
            dve.memset(KT[:, :, N:W1], 0.0)
            dve.memset(XT[:], 0.0)
            for u in range(2):
                dve.memset(cw[u][:, E:P], 0.0)
            dve.memset(CT[:], 0.0).then_inc(dve_consts, 1)
            dve.wait_ge(dve_consts, 1)
            dve.memset(SR[:, :, :, N:W1], 1.0).then_inc(s_done, 2)
            dve.wait_ge(weights_in, 16 * 13)

            def steady():
                dve.sem_inc(carried, 1)

            def normalise(u, src, n, done, per, j):
                if n == 1:
                    dve.bn_stats(st[u][:], src).then_inc(done, 1)
                elif n == 2:
                    dve.wait_ge(done, j * per + 1)
                    steady()
                    dve.bn_aggr(mv[u][:], st[u][:]).then_inc(done, 1)
                elif n == 3:
                    dve.wait_ge(done, j * per + 2)
                    dve.tensor_scalar(ve[u][:], mv[u][:, 1:2], LN_EPS, None, ALU.add).then_inc(done, 1)
                elif n == 4:
                    dve.tensor_scalar(xn[u][:], src, mv[u][:, 0:1], rstd[u][:], ALU.subtract, ALU.mult).then_inc(done, 1)

            def gate_step(u, j, n):
                src, done = (X2 if u else XA)[:], gd[u]
                if n == 1:
                    if u:
                        dve.wait_ge(x2_done, j + 1)
                    else:
                        dve.wait_ge(x_in, 32 * (j + 1))
                if n == 4:
                    dve.wait_ge(gp[u], j + 1)
                if n <= 4:
                    normalise(u, src, n, done, GD, j)
                elif n == 5:
                    dve.wait_ge(ga[u], j * GA + 2)
                    dve.tensor_tensor(biased[u][:], gate_ps[u][:, P:P + E], EB[:], ALU.add).then_inc(done, 1)
                elif n == 6:
                    dve.wait_ge(done, j * GD + 5)
                    steady()
                    dve.max(top8[u][:], biased[u][:]).then_inc(done, 1)
                elif n == 7:
                    dve.wait_ge(done, j * GD + 6)
                    steady()
                    dve.match_replace(rest[u][:], top8[u][:], biased[u][:], -3.0e38).then_inc(done, 1)
                elif n == 8:
                    dve.wait_ge(done, j * GD + 7)
                    dve.tensor_tensor(chosen[u][:], rest[u][:], biased[u][:], ALU.not_equal).then_inc(done, 1)
                elif n == 9:
                    dve.wait_ge(done, j * GD + 8)
                    dve.scalar_tensor_tensor(w2[u][:], th_aff[u][:], 1.0, chosen[u][:], ALU.add, ALU.mult).then_inc(done, 1)
                elif n == 10:
                    dve.wait_ge(done, j * GD + 9)
                    dve.tensor_reduce(wsum[u][:, 0:1], w2[u][:], AX.X, ALU.add).then_inc(done, 1)
                elif n == 11:
                    dve.wait_ge(done, j * GD + 10)
                    dve.tensor_scalar(wsum[u][:, 1:2], wsum[u][:, 0:1], 0.5, SUM_EPS, ALU.mult, ALU.add).then_inc(done, 1)
                elif n == 12:
                    dve.wait_ge(done, j * GD + 11)
                    dve.reciprocal(wsum[u][:, 2:3], wsum[u][:, 1:2]).then_inc(done, 1)
                elif n == 13:
                    dve.wait_ge(done, j * GD + 12)
                    dve.tensor_scalar(cw[u][:, 0:E], w2[u][:], wsum[u][:, 2:3], 0.5, ALU.mult, ALU.mult).then_inc(done, 1)

            def gate(k, e):
                dve.wait_ge(silu_done, k * CH + e + 1)
                if e >= DEEP:
                    dve.wait_ge(down_done, k * CH + e - DEEP + 1)
                dve.tensor_tensor(HG[:, e % DEEP, :, :].rearrange("p u t -> p (u t)"), HS[:, e % DEEP, :, :].rearrange("p u t -> p (u t)"),
                                  up_ps[e % DEEP][:, 256:512], ALU.mult).then_inc(gated, 1)

            def ffn_sums(k, has):
                dve.wait_ge(down_done, (k + 1) * CH)
                if has[0]:
                    if not isinstance(k, int) or k >= 1:
                        dve.tensor_copy(X1P[:], X1N[:]).then_inc(x1_done, 1)
                    else:
                        dve.memset(X1P[:], 0.0).then_inc(x1_done, 1)
                    dve.wait_ge(x1_done, 2 * k + 1)
                    dve.scalar_tensor_tensor(X1N[:], acc[0][:, 0:D], 0.5, XA[:], ALU.mult, ALU.add).then_inc(x1_done, 1)
                if has[2]:
                    if not isinstance(k, int) or k > 2:
                        dve.wait_ge(out_stored, 32 * (k - 2))
                    dve.scalar_tensor_tensor(OT[:], acc[1][:, 0:D], 0.5, X2[:], ALU.mult, ALU.add).then_inc(out_ready, 1)

            def cell_inputs(k, n):
                if n == 1:
                    dve.wait_ge(x1_done, 2 * k + 2)
                if n == 4:
                    dve.wait_ge(pp, k * PP + 1)
                if n <= 4:
                    normalise(2, X1N[:], n, pd, PD, k)
                elif n == 5:
                    dve.wait_ge(pa, k * PA + 3)
                    dve.tensor_reduce(KSS[:, 0, :], KSQ[:].rearrange("p (h n) -> p h n", h=HEADS), AX.X, ALU.add).then_inc(pd, 1)
                elif n == 6:
                    dve.wait_ge(pp, k * PP + 2)
                    dve.tensor_scalar(KSS[:, 2, :], KSS[:, 1, :], NORM_EPS, -1.0, ALU.add, ALU.mult).then_inc(pd, 1)
                elif n == 7:
                    dve.wait_ge(pd, k * PD + 6)
                    dve.reciprocal(KSS[:, 3, :], KSS[:, 2, :]).then_inc(pd, 1)
                elif n == 8:
                    if not isinstance(k, int) or k >= 1:
                        dve.wait_ge(k_stored, 64 * k)
                    dve.wait_ge(pa, k * PA + 4)
                    dve.wait_ge(pd, k * PD + 7)
                    dve.tensor_tensor(KT[:, :, 0:N], kq_ps[:, 0:M].rearrange("p (h n) -> p h n", h=HEADS),
                                      KSS[:, 3, :].unsqueeze(2).to_broadcast([P, HEADS, N]), ALU.mult).then_inc(pd, 1)
                elif n == 9:
                    dve.wait_ge(pa, k * PA + 7)
                    dve.tensor_scalar(BN[:], BN[:], 0.5, 0.5, ALU.mult, ALU.add).then_inc(pd, 1)

            def place_beta(j):
                dve.wait_ge(pd, (j + 1) * PD)
                dve.tensor_copy(BT[:], BN[:]).then_inc(beta_placed, 1)

            def place_v(j, r):
                dve.wait_ge(kb_in[r], 64 * (j + 1))
                dve.wait_ge(pa, j * PA + 5)
                for b in range(B):
                    steps = slice(GRP * r, GRP * r + GRP)
                    ins = dve.tensor_copy(KB[:, steps, 2 * b:2 * b + 2, N], VN[:, :, b, steps].rearrange("p h t -> p t h"))
                ins.then_inc(v_placed, 1)

            def n_of(j, t, h):
                return j * 2 * STEPS + 2 * t + h + 1

            def prod(j, t, h):
                if h == 0 and t % GRP == 0:
                    dve.wait_ge(v_placed, NGRP * j + t // GRP + 1)
                dve.wait_ge(s_done, n_of(j, t, h))
                dve.tensor_tensor(PR[:, g_of(h), :], SR[:, (t - 1) % RING, g_of(h), :], KB[:, t, g_of(h), :],
                                  ALU.mult).then_inc(prod_done, 1)

            def delta(j, t, h):
                dve.wait_ge(prod_done, n_of(j, t, h))
                dve.tensor_reduce(DEL[:, g_of(h)], PR[:, g_of(h), :], AX.X, ALU.add).then_inc(delta_done, 1)

            def outer(j, t, h):
                dve.wait_ge(delta_done, n_of(j, t, h))
                dve.tensor_tensor(WT[:, g_of(h), :], KB[:, t, g_of(h), 0:N],
                                  DEL[:, g_of(h)].unsqueeze(2).to_broadcast([P, 2, N]), ALU.mult).then_inc(outer_done, 1)

            def add(j, t, h):
                dve.wait_ge(outer_done, n_of(j, t, h))
                dve.wait_ge(bs_done, n_of(j, t, h))
                dve.tensor_tensor(UU[:, g_of(h), :], QS[:, g_of(h), :], WT[:, g_of(h), :], ALU.subtract).then_inc(u_done, 1)

            def times_q(j, t):
                if t % GRP == 0:
                    dve.wait_ge(qb_in[t // GRP], 64 * (j + 1))
                if t % HALF == 0 and (not isinstance(j, int) or j >= 1):
                    dve.wait_ge(sq_done, 2 * (j - 1) + t // HALF + 1)
                dve.wait_ge(s_done, n_of(j, t, 1) + 2)
                dve.tensor_tensor(PQ[:, t, :, :], SR[:, t % RING, :, 0:N], QB[:, t, :, :], ALU.mult).then_inc(pq_done, 1)

            def cell_output(j, x1, n):
                if n == 1:
                    dve.wait_ge(osilu_done, j + 1)
                    dve.tensor_tensor(CO[:].rearrange("p h b t -> p t b h"), SQS[:].rearrange("p t (b h) -> p t b h", b=B),
                                      cell_ps[:, 0:256].rearrange("p (t b h) -> p t b h", b=B, h=2), ALU.mult).then_inc(co_done, 1)
                else:
                    dve.wait_ge(y_done, j + 1)
                    dve.tensor_tensor(X2[:], cell_ps[:, 256:384], x1[:], ALU.add).then_inc(x2_done, 1)

            def background(k, has, slot):
                if has[2]:
                    for n in range(2):
                        if slot == CELL_OUT_DVE[n]:
                            cell_output(k - 2, X1N if isinstance(k, int) and k > TILES else X1P, n + 1)
                for n in range(GD):
                    if has[0] and slot == GATE_AT[0] + GATE_DVE[n]:
                        gate_step(0, k, n + 1)
                    if has[2] and slot == GATE_AT[1] + GATE_DVE[n]:
                        gate_step(1, k - 2, n + 1)
                for e in range(EC):
                    if slot == ffn_slot(e) + 2:
                        gate(k, e)
                if slot == SUMS_AT:
                    ffn_sums(k, has)
                for n in range(PD):
                    if has[0] and slot == INPUTS_AT + INPUTS_DVE[n]:
                        cell_inputs(k, n + 1)

            def iteration(k, has):
                j = k - 1
                if has[1]:
                    place_beta(j)
                    place_v(j, 0)
                for t in range(STEPS):
                    if has[1]:
                        if t % GRP == GRP - 2 and t + 2 < STEPS:
                            place_v(j, t // GRP + 1)
                        prod(j, t, 0)
                        if t:
                            add(j, t - 1, 1)
                        delta(j, t, 0)
                    background(k, has, 2 * t)
                    if has[1]:
                        outer(j, t, 0)
                        if t:
                            times_q(j, t - 1)
                        prod(j, t, 1)
                        add(j, t, 0)
                        delta(j, t, 1)
                    background(k, has, 2 * t + 1)
                    if has[1]:
                        outer(j, t, 1)
                if has[1]:
                    add(j, STEPS - 1, 1)
                    times_q(j, STEPS - 1)

            each_iteration(dve, iteration)


def kernel(L0_attn_x, L0_attn_W_in, L0_attn_W_k, L0_attn_W_v, L0_attn_W_q, L0_attn_W_beta, L0_attn_b_beta, L0_attn_W_out,
           L0_ffn_centroids, L0_ffn_expert_biases, L0_ffn_Ws_up, L0_ffn_Ws_down, L0_ffn_W_up, L0_ffn_W_down):
    import numpy as np
    import concourse.bacc as bacc
    from concourse.bass_utils import run_bass_kernel_spmd

    nc = bacc.Bacc("TRN2", target_bir_lowering=False, num_devices=1)
    laid_out = {
        "x": L0_attn_x, "w_in": L0_attn_W_in.T, "w_k": L0_attn_W_k.T, "w_v": L0_attn_W_v.T, "w_q": L0_attn_W_q.T,
        "w_beta": L0_attn_W_beta.T, "b_beta": L0_attn_b_beta.reshape(2, P).T, "w_out": L0_attn_W_out.T, "cent": L0_ffn_centroids.T,
        "ebias": L0_ffn_expert_biases, "ws_up": L0_ffn_Ws_up, "ws_down": L0_ffn_Ws_down, "w_up": L0_ffn_W_up,
        "w_down": L0_ffn_W_down,
    }
    arrays, args = {}, []
    for name, a in laid_out.items():
        a = np.ascontiguousarray(a)
        arrays[f"in_{name}"] = a
        args.append(nc.dram_tensor(f"in_{name}", a.shape, F32, kind="ExternalInput").ap())
    args.append(nc.dram_tensor("out_y", (B, T, D), F32, kind="ExternalOutput").ap())
    args.append(nc.dram_tensor("key_rows", (4, STEPS, G, W1), F32, kind="Internal").ap())
    args.append(nc.dram_tensor("query_rows", (4, STEPS, G, N), F32, kind="Internal").ap())
    macaron_program(nc, *args)
    r = run_bass_kernel_spmd(nc, [arrays], core_ids=[0])
    return r.results[0]["out_y"]
```

```python
from contextlib import ExitStack

import concourse.bass as bass
from concourse import mybir

F32 = mybir.dt.float32
ALU = mybir.AluOpType
ACT = mybir.ActivationFunctionType
AX = mybir.AxisListType

P = 128
D = 128
HEADS, N = 8, 32
M = HEADS * N
E, F = 64, 64
EC = E * F // P
B, T = 2, 1024
STEPS = 64
TILES = T // STEPS
G = 4
GRP = 16
NGRP = STEPS // GRP
RING = 32
HALF = STEPS // 2
W1 = N + 1
LN_EPS, NORM_EPS, SUM_EPS = 1e-5, 1e-6, 1e-8
QUARTERS = 4
DEEP = 4
CH = EC + 1

CELL_OUT_ACT, CELL_OUT_DVE = 28, (31, 40)
FFN_AT, FFN_SPAN, SUMS_AT = 0, 89, 94
GATE_LAG = 3
LAST_CELL = TILES
LAST_PASSES = ((0, 53, 59), (79, 42, 126))
LAST_ROUTE_DVE, LAST_ROUTE_ACT = (41, 42, 43, 45, 65, 66, 67, 68, 69, 70, 71, 72, 73), (60, 63, 76)
INPUTS_AT = SUMS_AT + 1
INPUTS_DVE = (0, 1, 2, 3, 12, 14, 15, 16, 18)
INPUTS_ACT = (4, 6, 11, 12, 13, 15, 16)
ROUTE_DVE = ((101, 102, 103, 107, 117, 118, 119, 120, 121, 122, 123, 124, 125),
             (40, 41, 42, 44, 102, 103, 104, 105, 106, 107, 108, 109, 110))
ROUTE_ACT = ((112, 115, 126), (97, 100, 114))
ROW_SUMS_AFTER, CELL_OUT_AFTER = ((23, 33), (0, 8)), 11
LAST_ROW_SUMS_AFTER, LAST_CELL_OUT_AFTER = ((2, 12), (18, 28)), 20


def passes(k):
    if isinstance(k, int) and k == LAST_CELL:
        return [(k + i, *LAST_PASSES[i]) for i in range(2)]
    if isinstance(k, int) and k == LAST_CELL + 1:
        return []
    return [(k, FFN_AT, FFN_SPAN, SUMS_AT)]


def silu_slot(first, span, e):
    return first + e * span // CH


def gate_slot(first, span, e, u):
    return first + GATE_LAG + (2 * e + u) * span // (2 * CH)


def route_slots(k):
    if isinstance(k, int) and k == LAST_CELL:
        return LAST_ROUTE_DVE, LAST_ROUTE_ACT
    return ROUTE_DVE[1], ROUTE_ACT[1]


GD, GT, GA = 13, 3, 3
PD, PP, PT, PA = 9, 2, 3, 7


def macaron_program(nc, x, w_in, w_k, w_v, w_q, w_beta, b_beta, w_out, cent, ebias, ws_up, ws_down, w_up, w_down,
                    out, key_rows, query_rows):
    with ExitStack() as ctx:
        def sb(name, shape):
            return ctx.enter_context(nc.sbuf_tensor(name, shape, F32))

        def ps(name):
            return ctx.enter_context(nc.psum_tensor(name, [P, 512], F32))

        def sem(name):
            return ctx.enter_context(nc.semaphore(name))

        WU = sb("WU", [P, EC, 2, F])
        WD = sb("WD", [P, EC, D])
        WSU = sb("WSU", [P, F])
        WSD = sb("WSD", [F, D])
        CENT = sb("CENT", [P, E])
        EB = sb("EB", [P, E])
        WIN = sb("WIN", [P, D])
        WK = sb("WK", [P, M])
        WQ = sb("WQ", [P, M])
        WV = sb("WV", [P, M])
        WB = sb("WB", [P, M])
        WO = sb("WO", [P, 2, D])
        BB = sb("BB", [P, 2])
        IDENT = sb("IDENT", [P, P])
        SEL = sb("SEL", [E, E, F])
        POW = sb("POW", [P, 16])
        XA = sb("XA", [P, D])
        X1N = sb("X1N", [P, D])
        X1P = sb("X1P", [P, D])
        X2 = sb("X2", [P, D])
        X2P = sb("X2P", [P, D])
        OT = sb("OT", [P, D])
        XT = sb("XT", [P, 2, P])
        CT = sb("CT", [E, 2, P])
        HS = sb("HS", [P, DEEP, 2, P])
        HG = sb("HG", [P, DEEP, 2, P])
        HSH = sb("HSH", [F, 2, P])
        st = [sb(f"st{u}", [P, 6]) for u in range(3)]
        mv = [sb(f"mv{u}", [P, 2]) for u in range(3)]
        ve = [sb(f"ve{u}", [P, 1]) for u in range(3)]
        rstd = [sb(f"rstd{u}", [P, 1]) for u in range(3)]
        xn = [sb(f"xn{u}", [P, D]) for u in range(3)]
        biased = [sb(f"biased{u}", [P, E]) for u in range(2)]
        top8 = [sb(f"top8{u}", [P, 8]) for u in range(2)]
        rest = [sb(f"rest{u}", [P, E]) for u in range(2)]
        chosen = [sb(f"chosen{u}", [P, E]) for u in range(2)]
        th_aff = [sb(f"th_aff{u}", [P, E]) for u in range(2)]
        w2 = [sb(f"w2{u}", [P, E]) for u in range(2)]
        wsum = [sb(f"wsum{u}", [P, 3]) for u in range(2)]
        cw = [sb(f"cw{u}", [P, P]) for u in range(2)]
        XNT = sb("XNT", [P, P])
        XP = sb("XP", [P, P])
        KSQ = sb("KSQ", [P, M])
        KSS = sb("KSS", [P, 4, HEADS])
        KT = sb("KT", [P, HEADS, W1])
        QT = sb("QT", [P, M])
        VN = sb("VN", [P, 2, B, STEPS])
        BN = sb("BN", [P, 2, B, STEPS])
        BT = sb("BT", [P, 2, B, STEPS])
        KB = sb("KB", [P, STEPS, G, W1])
        QB = sb("QB", [P, STEPS, G, N])
        SR = sb("SR", [P, RING, G, W1])
        PR = sb("PR", [P, G, W1])
        DEL = sb("DEL", [P, G])
        WT = sb("WT", [P, G, N])
        QS = sb("QS", [P, G, N])
        UU = sb("UU", [P, G, N])
        PQ = sb("PQ", [P, STEPS, G, N])
        SQS = sb("SQS", [P, STEPS, G])
        CO = sb("CO", [P, 2, B, STEPS])

        acc = [ps("acc0"), ps("acc1")]
        cell_ps = ps("cell_ps")
        kq_ps = ps("kq_ps")
        vb_ps = ps("vb_ps")
        up_ps = [ps("up0"), ps("up1"), kq_ps, vb_ps]
        gate_ps = [ps("gate_ps"), up_ps[0]]

        route_weights_in, weights_in = sem("route_weights_in"), sem("weights_in")
        experts_in = [sem(f"experts_in{q}") for q in range(QUARTERS)]
        pool_consts, dve_consts = sem("pool_consts"), sem("dve_consts")
        selectors_built = sem("selectors_built")
        x_in = sem("x_in")
        gd = [sem("gd0"), sem("gd1")]
        gp = [sem("gp0"), sem("gp1")]
        gt = [sem("gt0"), sem("gt1")]
        ga = [sem("ga0"), sem("ga1")]
        up_done, silu_done, gated, down_done = sem("up_done"), sem("silu_done"), sem("gated"), sem("down_done")
        x1_done, out_ready, out_stored = sem("x1_done"), sem("out_ready"), sem("out_stored")
        pd, pp, pt, pa = sem("pd"), sem("pp"), sem("pt"), sem("pa")
        k_stored, q_stored, v_placed, beta_placed = (sem(s) for s in ("k_stored", "q_stored", "v_placed", "beta_placed"))
        kb_in = [sem(f"kb_in{r}") for r in range(NGRP)]
        qb_in = [sem(f"qb_in{r}") for r in range(NGRP)]
        prod_done, delta_done, outer_done, u_done, s_done, bs_done, pq_done = (sem(s) for s in (
            "prod_done", "delta_done", "outer_done", "u_done", "s_done", "bs_done", "pq_done"))
        sq_done, osilu_done, co_done, y_done, x2_done = (sem(s) for s in (
            "sq_done", "osilu_done", "co_done", "y_done", "x2_done"))

        x2_moved = sem("x2_moved")
        third_quarter_summed = sem("third_quarter_summed")
        carried = sem("carried")

        def each_iteration(eng, body):
            for k in range(3):
                body(k)
            with eng.Fori(3, TILES - 1) as k:
                body(k)
            for k in range(TILES - 1, TILES + 3):
                body(k)

        def there(j):
            return not isinstance(j, int) or 0 <= j < TILES

        def ffns(k):
            return [u for u, j in ((0, k), (1, k - 3)) if there(j)]

        def g_of(h):
            return slice(2 * h, 2 * h + 2)

        block = ctx.enter_context(nc.Block())

        @block.sync
        def _(sp):
            for dst, src in ((CENT[:], cent), (EB[:], ebias.partition_broadcast(P)), (BB[:], b_beta)):
                sp.dma_start(dst, src).then_inc(route_weights_in, 16)
            sp.dma_start(XA[0:STEPS, :], x[0, 0:STEPS, :]).then_inc(x_in, 16)
            sp.dma_start(XA[STEPS:P, :], x[1, 0:STEPS, :]).then_inc(x_in, 16)
            w_up_rows = w_up.rearrange("(c m) d f -> d c m f", m=2)
            w_down_rows = w_down.rearrange("(c m) f d -> (m f) c d", m=2)
            for q in range(QUARTERS):
                chunks = slice(q * EC // QUARTERS, (q + 1) * EC // QUARTERS)
                sp.dma_start(WU[:, chunks], w_up_rows[:, chunks]).then_inc(experts_in[q], 16)
                sp.dma_start(WD[:, chunks], w_down_rows[:, chunks]).then_inc(experts_in[q], 16)
            for dst, src in ((WSU[:], ws_up), (WSD[:], ws_down), (WIN[:], w_in), (WK[:], w_k), (WQ[:], w_q),
                             (WV[:], w_v), (WB[:], w_beta), (WO[:], w_out.rearrange("(h p) d -> p h d", h=2))):
                sp.dma_start(dst, src).then_inc(weights_in, 16)

            def iteration(k):
                if there(k + 1) and there(k):
                    sp.wait_ge(x1_done, 2 * k + 2)
                    sp.sem_inc(carried, 1)
                    for b in range(B):
                        sp.dma_start(XA[b * STEPS:(b + 1) * STEPS, :],
                                     x[b, bass.ds((k + 1) * STEPS, STEPS), :]).then_inc(x_in, 16)
                if there(k - 3):
                    sp.wait_ge(out_ready, k - 2)
                    sp.sem_inc(carried, 1)
                    for b in range(B):
                        sp.dma_start(out[b, bass.ds((k - 3) * STEPS, STEPS), :],
                                     OT[b * STEPS:(b + 1) * STEPS, :]).then_inc(out_stored, 16)
                if there(k):
                    for done, count, rows_dram, width, src, stored in (
                            (pa, k * PA + 4, query_rows, N, QT[:].rearrange("p (h w) -> p h w", w=N), q_stored),
                            (pd, k * PD + 8, key_rows, W1, KT[:], k_stored)):
                        sp.wait_ge(done, count)
                        for b in range(B):
                            dst = rows_dram.rearrange("s t (b h) w -> b t h s w", b=B)[b]
                            for h in range(2):
                                sp.dma_start(dst[:, h], src[b * STEPS:(b + 1) * STEPS, 4 * h:4 * h + 4, :]).then_inc(stored, 16)
                    sp.wait_ge(k_stored, 64 * (k + 1))
                    sp.wait_ge(q_stored, 64 * (k + 1))
                    for r in range(NGRP):
                        if there(k - 1):
                            sp.wait_ge(pq_done, (k - 1) * STEPS + GRP * (r + 1))
                        for rows_dram, dst, arrived in ((key_rows, KB, kb_in[r]), (query_rows, QB, qb_in[r])):
                            for s in range(4):
                                steps = slice(GRP * r, GRP * r + GRP)
                                sp.dma_start(dst[N * s:N * s + N, steps, :, :].rearrange("p t g w -> p (t g w)"),
                                             rows_dram[s, steps].rearrange("t g w -> (t g w)").partition_broadcast(N)).then_inc(arrived, 16)
                    for r in range(NGRP):
                        sp.wait_ge(kb_in[r], 64 * (k + 1))
                        sp.wait_ge(qb_in[r], 64 * (k + 1))
                    sp.sem_inc(carried, 1)

            each_iteration(sp, iteration)
            sp.wait_ge(out_stored, 32 * TILES)

        @block.gpsimd
        def _(pool):
            pool.memset(IDENT[:], 0.0).then_inc(pool_consts, 1)
            pool.memset(POW[:, 0:8], -0.5)
            pool.memset(POW[:, 8:16], 0.5).then_inc(pool_consts, 1)
            pool.wait_ge(pool_consts, 2)
            pool.affine_select(out=IDENT[:], in_=IDENT[:], compare_op=ALU.not_equal, fill=1.0, base=0,
                               pattern=[[-1, P]], channel_multiplier=1).then_inc(pool_consts, 1)
            pool.wait_ge(pool_consts, 3)

            def route(u, j):
                pool.wait_ge(gd[u], j * GD + 3)
                pool.tensor_tensor(rstd[u][:], ve[u][:], POW[:, 0:1], ALU.pow).then_inc(gp[u], 1)

            def iteration(k):
                if there(k - 2):
                    route(1, k - 2)
                if there(k):
                    pool.wait_ge(pd, k * PD + 3)
                    pool.tensor_tensor(rstd[2][:], ve[2][:], POW[:, 0:1], ALU.pow).then_inc(pp, 1)
                if there(k) and there(k + 1):
                    route(0, k + 1)
                if there(k):
                    pool.wait_ge(pd, k * PD + 5)
                    pool.tensor_tensor(KSS[:, 1, :], KSS[:, 0, :], POW[:, 8:16], ALU.pow).then_inc(pp, 1)

            route(0, 0)
            each_iteration(pool, iteration)

        @block.tensor
        def _(pe):
            pe.wait_ge(route_weights_in, 16 * 3)
            pe.wait_ge(pool_consts, 3)
            pe.wait_ge(dve_consts, 2)

            def gate_step(u, j, n):
                if n == 1:
                    pe.wait_ge(gd[u], j * GD + 4)
                    pe.transpose(gate_ps[u][:, 0:P], xn[u][:], IDENT[:]).then_inc(gt[u], 1)
                elif n == 2:
                    pe.wait_ge(ga[u], j * GA + 1)
                    pe.matmul(gate_ps[u][:, P:P + E], XT[:, u, :], CENT[:], start=True, stop=True).then_inc(gt[u], 1)
                elif n == 3:
                    pe.wait_ge(gd[u], j * GD + 13)
                    pe.transpose(gate_ps[u][:, 0:P], cw[u][:], IDENT[:]).then_inc(gt[u], 1)

            def up(k, e):
                us = ffns(k)
                cols, both = slice(P * us[0], P * us[-1] + P), slice(us[0], us[-1] + 1)
                if e >= DEEP:
                    pe.wait_ge(silu_done, k * CH + e - DEEP + 1)
                    pe.wait_ge(gated, 2 * (k * EC + e - DEEP + 1))
                if isinstance(k, int) and k == 0:
                    if e == EC:
                        pe.wait_ge(weights_in, 16 * 8)
                    elif e % (EC // QUARTERS) == 0:
                        pe.wait_ge(experts_in[e * QUARTERS // EC], 32)
                if e < EC:
                    pe.matmul(up_ps[e % DEEP][:, cols], WU[:, e, :, :], XT[:, both, :], start=True, stop=True)
                    pe.matmul(up_ps[e % DEEP][:, 256 + cols.start:256 + cols.stop], SEL[:, 2 * e:2 * e + 2, :],
                              CT[:, both, :], start=True, stop=True).then_inc(up_done, 1)
                else:
                    pe.matmul(up_ps[e % DEEP][0:F, cols], WSU[:], XT[:, both, :], start=True, stop=True).then_inc(up_done, 1)

            def down(k, e):
                us = ffns(k)
                if e == EC:
                    pe.wait_ge(silu_done, k * CH + e + 1)
                for u in us:
                    if e < EC:
                        pe.wait_ge(gated, 2 * (k * EC + e) + (u + 1 if len(us) == 2 else 2))
                        ins = pe.matmul(acc[u][:, 0:D], HG[:, e % DEEP, u, :], WD[:, e, :], start=(e == 0), stop=False)
                    else:
                        ins = pe.matmul(acc[u][:, 0:D], HSH[:, u, :], WSD[:], start=False, stop=True)
                ins.then_inc(down_done, 1)

            def cell_inputs(k, n):
                if n == 1:
                    pe.wait_ge(pd, k * PD + 4)
                    pe.transpose(cell_ps[:, 384:512], xn[2][:], IDENT[:]).then_inc(pt, 1)
                elif n == 2:
                    pe.wait_ge(pa, k * PA + 1)
                    pe.matmul(gate_ps[0][:, 384:512], WIN[:], XNT[:], start=True, stop=True).then_inc(pt, 1)
                elif n == 3:
                    pe.wait_ge(pa, k * PA + 2)
                    pe.matmul(kq_ps[:, 0:M], XP[:], WK[:], start=True, stop=True)
                    pe.matmul(kq_ps[:, M:2 * M], XP[:], WQ[:], start=True, stop=True)
                    for h in range(2):
                        pe.matmul(vb_ps[:, P * h:P * h + P], WV[:, P * h:P * h + P], XP[:], start=True, stop=True)
                        ins = pe.matmul(vb_ps[:, M + P * h:M + P * h + P], WB[:, P * h:P * h + P], XP[:], start=True, stop=True)
                    ins.then_inc(pt, 1)

            def row_sums(j, first, steps, part=0, parts=1):
                if part == 0:
                    pe.wait_ge(pq_done, j * STEPS + first + steps)
                for c in range(part * N // parts, (part + 1) * N // parts):
                    ins = pe.matmul(cell_ps[:, G * first:G * (first + steps)],
                                    IDENT[:], PQ[:, first:first + steps, :, c],
                                    start=(c == 0), stop=(c == N - 1))
                if part == parts - 1:
                    ins.then_inc(sq_done if steps == HALF else third_quarter_summed, 1)

            def cell_output(j):
                pe.wait_ge(co_done, j + 1)
                for h in range(2):
                    ins = pe.matmul(cell_ps[:, 256:384], CO[:, h, :, :], WO[:, h, :],
                                    start=(h == 0), stop=(h == 1))
                ins.then_inc(y_done, 1)

            def start_pass(k):
                if there(k - 3):
                    pe.wait_ge(ga[1], (k - 2) * GA)
                if there(k):
                    pe.wait_ge(ga[0], (k + 1) * GA)
                if there(k - 1):
                    pe.wait_ge(pd, (k - 1) * PD + 8)
                    pe.wait_ge(pa, (k - 1) * PA + 7)
                for e in range(DEEP):
                    up(k, e)

            def chunk(k, e):
                down(k, e)
                if e + DEEP < CH:
                    up(k, e + DEEP)

            def sums_part(j, after, e, first, steps):
                if there(j) and after[0] <= e < after[1]:
                    row_sums(j, first, steps, e - after[0], after[1] - after[0])

            def iteration(k):
                last = isinstance(k, int) and k == LAST_CELL
                in_pass = ffns(k) and passes(k)
                if in_pass:
                    start_pass(k)
                for e in range(CH):
                    if in_pass:
                        chunk(k, e)
                    if not isinstance(k, int) or k != LAST_CELL + 1:
                        sums_part(k - 2, ROW_SUMS_AFTER[1], e, HALF, HALF)
                    if not last:
                        sums_part(k - 1, ROW_SUMS_AFTER[0], e, 0, HALF)
                    if there(k - 2) and e == (LAST_CELL_OUT_AFTER if last else CELL_OUT_AFTER):
                        cell_output(k - 2)
                if there(k - 2):
                    gate_step(1, k - 2, 1)
                    gate_step(1, k - 2, 2)
                if last:
                    gate_step(1, k - 2, 3)
                    start_pass(k + 1)
                    for e in range(CH):
                        chunk(k + 1, e)
                        sums_part(k - 1, LAST_ROW_SUMS_AFTER[0], e, 0, HALF)
                        sums_part(k - 1, LAST_ROW_SUMS_AFTER[1], e, HALF, HALF // 2)
                if there(k):
                    cell_inputs(k, 1)
                    cell_inputs(k, 2)
                    cell_inputs(k, 3)
                    if there(k + 1):
                        gate_step(0, k + 1, 1)
                        gate_step(0, k + 1, 2)
                if there(k - 2) and not last:
                    gate_step(1, k - 2, 3)
                if there(k) and there(k + 1):
                    gate_step(0, k + 1, 3)

            for n in (1, 2, 3):
                gate_step(0, 0, n)
            pe.wait_ge(selectors_built, 1)
            each_iteration(pe, iteration)

        @block.scalar
        def _(act):
            act.preload_act_table_set("silu_and_others")
            act.wait_ge(route_weights_in, 16 * 3)
            act.wait_ge(dve_consts, 2)

            def gate_step(u, j, n):
                if n == 1:
                    act.wait_ge(gt[u], j * GT + 1)
                    act.copy(XT[:, u, :], gate_ps[u][:, 0:P]).then_inc(ga[u], 1)
                elif n == 2:
                    act.wait_ge(gt[u], j * GT + 2)
                    act.activation(th_aff[u][:], gate_ps[u][:, P:P + E], ACT.Tanh, scale=0.5).then_inc(ga[u], 1)
                elif n == 3:
                    act.wait_ge(gt[u], j * GT + 3)
                    act.copy(CT[:, u, :], gate_ps[u][0:E, 0:P]).then_inc(ga[u], 1)

            def silu(k, e):
                us = ffns(k)
                cols, both = slice(P * us[0], P * us[-1] + P), slice(us[0], us[-1] + 1)
                act.wait_ge(up_done, k * CH + e + 1)
                if e < EC:
                    if e >= DEEP:
                        act.wait_ge(gated, 2 * (k * EC + e - DEEP + 1))
                    act.activation(HS[:, e % DEEP, both, :], up_ps[e % DEEP][:, cols], ACT.Silu).then_inc(silu_done, 1)
                else:
                    act.activation(HSH[:, both, :], up_ps[e % DEEP][0:F, cols], ACT.Silu).then_inc(silu_done, 1)

            def cell_inputs(k, n):
                if n == 1:
                    act.wait_ge(pt, k * PT + 1)
                    act.copy(XNT[:], cell_ps[:, 384:512]).then_inc(pa, 1)
                elif n == 2:
                    act.wait_ge(pt, k * PT + 2)
                    act.activation(XP[:], gate_ps[0][:, 384:512], ACT.Silu).then_inc(pa, 1)
                elif n == 3:
                    act.wait_ge(pt, k * PT + 3)
                    act.activation(KSQ[:], kq_ps[:, 0:M], ACT.Square).then_inc(pa, 1)
                elif n == 4:
                    if not isinstance(k, int) or k >= 1:
                        act.wait_ge(q_stored, 64 * k)
                    act.copy(QT[:], kq_ps[:, M:2 * M]).then_inc(pa, 1)
                elif n == 5:
                    if not isinstance(k, int) or k >= 1:
                        act.wait_ge(v_placed, NGRP * k)
                    act.copy(VN[:].rearrange("p h b t -> p (h b t)"), vb_ps[:, 0:M]).then_inc(pa, 1)
                elif n in (6, 7):
                    h = n - 6
                    if n == 6 and (not isinstance(k, int) or k >= 1):
                        act.wait_ge(beta_placed, k)
                    act.activation(BN[:, h, :, :].rearrange("p b t -> p (b t)"), vb_ps[:, M + P * h:M + P * h + P], ACT.Tanh,
                                   bias=HB[:, h:h + 1], scale=0.5).then_inc(pa, 1)

            HB = sb("HB", [P, 2])
            half_bias = sem("half_bias")
            act.mul(HB[:], BB[:], 0.5).then_inc(half_bias, 1)
            act.wait_ge(half_bias, 1)

            def place_beta(j):
                act.wait_ge(pd, (j + 1) * PD)
                act.wait_ge(bs_done, 2 * STEPS * j + 2)
                act.copy(BT[:, :, :, 1:STEPS], BN[:, :, :, 1:STEPS]).then_inc(beta_placed, 1)

            def place_v(j, r):
                act.wait_ge(pa, j * PA + 5)
                act.wait_ge(kb_in[r], 64 * (j + 1))
                for b in range(B):
                    steps = slice(GRP * r, GRP * r + GRP)
                    ins = act.copy(KB[:, steps, 2 * b:2 * b + 2, N], VN[:, :, b, steps].rearrange("p h t -> p t h"))
                ins.then_inc(v_placed, 1)

            def decayed(j, t, h):
                if t == 0 and h == 0:
                    act.wait_ge(pd, (j + 1) * PD)
                elif t == 1 and h == 0:
                    act.wait_ge(beta_placed, j + 1)
                beta = BN if t == 0 else BT
                act.wait_ge(s_done, j * 2 * STEPS + 2 * t + h + 1)
                for hh in range(2):
                    g = 2 * h + hh
                    ins = act.activation(QS[:, g, :], SR[:, (t - 1) % RING, g, 0:N], ACT.Identity,
                                         scale=beta[:, hh, h, t:t + 1])
                ins.then_inc(bs_done, 1)

            def new_state(j, t, h):
                act.wait_ge(u_done, j * 2 * STEPS + 2 * t + h + 1)
                act.activation(SR[:, t % RING, g_of(h), 0:N], UU[:, g_of(h), :], ACT.Tanh).then_inc(s_done, 1)

            def background(k, slot):
                if there(k - 2) and slot == CELL_OUT_ACT:
                    act.wait_ge(sq_done, 2 * (k - 1))
                    act.activation(SQS[:].rearrange("p t g -> p (t g)"), cell_ps[:, 0:256], ACT.Silu).then_inc(osilu_done, 1)
                if ffns(k):
                    for number, first, span, sums_at in passes(k):
                        for e in range(CH):
                            if slot == silu_slot(first, span, e):
                                silu(number, e)
                for n in range(GA):
                    if there(k - 2) and slot == route_slots(k)[1][n]:
                        gate_step(1, k - 2, n + 1)
                    if there(k) and there(k + 1) and slot == ROUTE_ACT[0][n]:
                        gate_step(0, k + 1, n + 1)
                for n in range(PA):
                    if there(k) and slot == INPUTS_AT + INPUTS_ACT[n]:
                        cell_inputs(k, n + 1)

            def iteration(k):
                if isinstance(k, int) and k == 1:
                    place_v(0, 0)
                    for h in range(2):
                        decayed(0, 0, h)
                for t in range(STEPS):
                    for h in range(2):
                        if there(k - 1):
                            new_state(k - 1, t, h)
                            if t == 0 and h == 0:
                                place_beta(k - 1)
                            if t % GRP == GRP - 2 and h == 1:
                                if t + 2 < STEPS:
                                    place_v(k - 1, t // GRP + 1)
                                elif there(k):
                                    place_v(k, 0)
                        background(k, 2 * t + h)
                        if there(k - 1) and t + 1 < STEPS:
                            decayed(k - 1, t + 1, h)
                        elif there(k - 1) and there(k):
                            decayed(k, 0, h)

            gate_step(0, 0, 1)
            gate_step(0, 0, 2)
            act.wait_ge(pool_consts, 3)
            act.copy(SEL[:], IDENT[0:E, 0:E].unsqueeze(2).to_broadcast([E, E, F])).then_inc(selectors_built, 1)
            gate_step(0, 0, 3)
            each_iteration(act, iteration)

        @block.vector
        def _(dve):
            dve.memset(SR[:], 0.0).then_inc(dve_consts, 1)
            dve.memset(KT[:, :, N:W1], 0.0)
            dve.memset(XT[:], 0.0)
            for u in range(2):
                dve.memset(cw[u][:, E:P], 0.0)
            dve.memset(CT[:], 0.0).then_inc(dve_consts, 1)
            dve.wait_ge(dve_consts, 1)
            dve.memset(SR[:, :, :, N:W1], 1.0).then_inc(s_done, 2)
            dve.wait_ge(route_weights_in, 16 * 3)

            def steady():
                dve.sem_inc(carried, 1)

            def normalise(u, src, n, done, per, j):
                if n == 1:
                    dve.bn_stats(st[u][:], src).then_inc(done, 1)
                elif n == 2:
                    dve.wait_ge(done, j * per + 1)
                    steady()
                    dve.bn_aggr(mv[u][:], st[u][:]).then_inc(done, 1)
                elif n == 3:
                    dve.wait_ge(done, j * per + 2)
                    dve.tensor_scalar(ve[u][:], mv[u][:, 1:2], LN_EPS, None, ALU.add).then_inc(done, 1)
                elif n == 4:
                    dve.tensor_scalar(xn[u][:], src, mv[u][:, 0:1], rstd[u][:], ALU.subtract, ALU.mult).then_inc(done, 1)

            def gate_step(u, j, n):
                src, done = (X2 if u else XA)[:], gd[u]
                if n == 1:
                    if u:
                        dve.wait_ge(x2_done, j + 1)
                    else:
                        dve.wait_ge(x_in, 32 * (j + 1))
                if n == 4:
                    dve.wait_ge(gp[u], j + 1)
                if n <= 4:
                    normalise(u, src, n, done, GD, j)
                elif n == 5:
                    dve.wait_ge(ga[u], j * GA + 2)
                    dve.tensor_tensor(biased[u][:], gate_ps[u][:, P:P + E], EB[:], ALU.add).then_inc(done, 1)
                elif n == 6:
                    dve.wait_ge(done, j * GD + 5)
                    steady()
                    dve.max(top8[u][:], biased[u][:]).then_inc(done, 1)
                elif n == 7:
                    dve.wait_ge(done, j * GD + 6)
                    steady()
                    dve.match_replace(rest[u][:], top8[u][:], biased[u][:], -3.0e38).then_inc(done, 1)
                elif n == 8:
                    dve.wait_ge(done, j * GD + 7)
                    dve.tensor_tensor(chosen[u][:], rest[u][:], biased[u][:], ALU.not_equal).then_inc(done, 1)
                elif n == 9:
                    dve.wait_ge(done, j * GD + 8)
                    dve.scalar_tensor_tensor(w2[u][:], th_aff[u][:], 1.0, chosen[u][:], ALU.add, ALU.mult).then_inc(done, 1)
                elif n == 10:
                    dve.wait_ge(done, j * GD + 9)
                    dve.tensor_reduce(wsum[u][:, 0:1], w2[u][:], AX.X, ALU.add).then_inc(done, 1)
                elif n == 11:
                    dve.wait_ge(done, j * GD + 10)
                    dve.tensor_scalar(wsum[u][:, 1:2], wsum[u][:, 0:1], 0.5, SUM_EPS, ALU.mult, ALU.add).then_inc(done, 1)
                elif n == 12:
                    dve.wait_ge(done, j * GD + 11)
                    dve.reciprocal(wsum[u][:, 2:3], wsum[u][:, 1:2]).then_inc(done, 1)
                elif n == 13:
                    dve.wait_ge(done, j * GD + 12)
                    dve.tensor_scalar(cw[u][:, 0:E], w2[u][:], wsum[u][:, 2:3], 0.5, ALU.mult, ALU.mult).then_inc(done, 1)

            def gate(k, e, u):
                if u == ffns(k)[0]:
                    dve.wait_ge(silu_done, k * CH + e + 1)
                if e >= DEEP:
                    dve.wait_ge(down_done, k * CH + e - DEEP + 1)
                dve.tensor_tensor(HG[:, e % DEEP, u, :], HS[:, e % DEEP, u, :], up_ps[e % DEEP][:, 256 + P * u:256 + P * u + P],
                                  ALU.mult).then_inc(gated, 2 // len(ffns(k)))

            def ffn_sums(k):
                dve.wait_ge(down_done, (k + 1) * CH)
                if there(k):
                    if not isinstance(k, int) or k >= 1:
                        dve.tensor_copy(X1P[:], X1N[:]).then_inc(x1_done, 1)
                    else:
                        dve.memset(X1P[:], 0.0).then_inc(x1_done, 1)
                    dve.wait_ge(x1_done, 2 * k + 1)
                    dve.scalar_tensor_tensor(X1N[:], acc[0][:, 0:D], 0.5, XA[:], ALU.mult, ALU.add).then_inc(x1_done, 1)
                if there(k - 3):
                    if not isinstance(k, int) or k > 3:
                        dve.wait_ge(out_stored, 32 * (k - 3))
                    x2 = X2 if isinstance(k, int) and k - 3 >= TILES - 2 else X2P
                    dve.scalar_tensor_tensor(OT[:], acc[1][:, 0:D], 0.5, x2[:], ALU.mult, ALU.add).then_inc(out_ready, 1)

            def cell_inputs(k, n):
                if n == 1:
                    dve.wait_ge(x1_done, 2 * k + 2)
                if n == 4:
                    dve.wait_ge(pp, k * PP + 1)
                if n <= 4:
                    normalise(2, X1N[:], n, pd, PD, k)
                elif n == 5:
                    dve.wait_ge(pa, k * PA + 3)
                    dve.tensor_reduce(KSS[:, 0, :], KSQ[:].rearrange("p (h n) -> p h n", h=HEADS), AX.X, ALU.add).then_inc(pd, 1)
                elif n == 6:
                    dve.wait_ge(pp, k * PP + 2)
                    dve.tensor_scalar(KSS[:, 2, :], KSS[:, 1, :], NORM_EPS, -1.0, ALU.add, ALU.mult).then_inc(pd, 1)
                elif n == 7:
                    dve.wait_ge(pd, k * PD + 6)
                    dve.reciprocal(KSS[:, 3, :], KSS[:, 2, :]).then_inc(pd, 1)
                elif n == 8:
                    if not isinstance(k, int) or k >= 1:
                        dve.wait_ge(k_stored, 64 * k)
                    dve.wait_ge(pa, k * PA + 4)
                    dve.wait_ge(pd, k * PD + 7)
                    dve.tensor_tensor(KT[:, :, 0:N], kq_ps[:, 0:M].rearrange("p (h n) -> p h n", h=HEADS),
                                      KSS[:, 3, :].unsqueeze(2).to_broadcast([P, HEADS, N]), ALU.mult).then_inc(pd, 1)
                elif n == 9:
                    dve.wait_ge(pa, k * PA + 7)
                    dve.tensor_scalar(BN[:], BN[:], 0.5, 0.5, ALU.mult, ALU.add).then_inc(pd, 1)

            def n_of(j, t, h):
                return j * 2 * STEPS + 2 * t + h + 1

            def prod(j, t, h):
                if h == 0 and t % GRP == 0:
                    dve.wait_ge(v_placed, NGRP * j + t // GRP + 1)
                dve.wait_ge(s_done, n_of(j, t, h))
                dve.tensor_tensor(PR[:, g_of(h), :], SR[:, (t - 1) % RING, g_of(h), :], KB[:, t, g_of(h), :],
                                  ALU.mult).then_inc(prod_done, 1)

            def delta(j, t, h):
                dve.wait_ge(prod_done, n_of(j, t, h))
                dve.tensor_reduce(DEL[:, g_of(h)], PR[:, g_of(h), :], AX.X, ALU.add).then_inc(delta_done, 1)

            def outer(j, t, h):
                dve.wait_ge(delta_done, n_of(j, t, h))
                dve.tensor_tensor(WT[:, g_of(h), :], KB[:, t, g_of(h), 0:N],
                                  DEL[:, g_of(h)].unsqueeze(2).to_broadcast([P, 2, N]), ALU.mult).then_inc(outer_done, 1)

            def add(j, t, h):
                dve.wait_ge(outer_done, n_of(j, t, h))
                dve.wait_ge(bs_done, n_of(j, t, h))
                dve.tensor_tensor(UU[:, g_of(h), :], QS[:, g_of(h), :], WT[:, g_of(h), :], ALU.subtract).then_inc(u_done, 1)

            def times_q(j, t):
                if t % GRP == 0:
                    dve.wait_ge(qb_in[t // GRP], 64 * (j + 1))
                if t % HALF == 0 and (not isinstance(j, int) or j >= 1):
                    dve.wait_ge(sq_done, 2 * (j - 1) + t // HALF + 1)
                dve.wait_ge(s_done, n_of(j, t, 1) + 2)
                dve.tensor_tensor(PQ[:, t, :, :], SR[:, t % RING, :, 0:N], QB[:, t, :, :], ALU.mult).then_inc(pq_done, 1)

            def last_row_sums(j):
                quarter = 3 * STEPS // 4
                dve.wait_ge(pq_done, (j + 1) * STEPS)
                dve.wait_ge(third_quarter_summed, 1)
                dve.tensor_reduce(cell_ps[:, G * quarter:G * STEPS], PQ[:, quarter:STEPS, :, :].rearrange("p t g w -> p (t g) w"),
                                  AX.X, ALU.add).then_inc(sq_done, 1)

            def cell_output(j, x1, n):
                if n == 1:
                    dve.wait_ge(osilu_done, j + 1)
                    dve.tensor_tensor(CO[:].rearrange("p h b t -> p t b h"), SQS[:].rearrange("p t (b h) -> p t b h", b=B),
                                      cell_ps[:, 0:256].rearrange("p (t b h) -> p t b h", b=B, h=2), ALU.mult).then_inc(co_done, 1)
                else:
                    dve.wait_ge(y_done, j + 1)
                    if not isinstance(j, int) or j >= 1:
                        dve.tensor_copy(X2P[:], X2[:]).then_inc(x2_moved, 1)
                        dve.wait_ge(x2_moved, j)
                    dve.tensor_tensor(X2[:], cell_ps[:, 256:384], x1[:], ALU.add).then_inc(x2_done, 1)

            def background(k, slot):
                for n in range(2):
                    if there(k - 2) and slot == CELL_OUT_DVE[n]:
                        cell_output(k - 2, X1N if isinstance(k, int) and k > TILES else X1P, n + 1)
                if ffns(k):
                    for number, first, span, sums_at in passes(k):
                        for e in range(EC):
                            for u in ffns(number):
                                if slot == gate_slot(first, span, e, u):
                                    gate(number, e, u)
                        if slot == sums_at:
                            ffn_sums(number)
                for n in range(GD):
                    if there(k - 2) and slot == route_slots(k)[0][n]:
                        gate_step(1, k - 2, n + 1)
                    if there(k) and there(k + 1) and slot == ROUTE_DVE[0][n]:
                        gate_step(0, k + 1, n + 1)
                for n in range(PD):
                    if there(k) and slot == INPUTS_AT + INPUTS_DVE[n]:
                        cell_inputs(k, n + 1)

            def iteration(k):
                j = k - 1
                if there(j - 1) and not there(j):
                    add(j - 1, STEPS - 1, 1)
                    times_q(j - 1, STEPS - 1)
                    last_row_sums(j - 1)
                for t in range(STEPS):
                    before = (j, t - 1) if t else (j - 1, STEPS - 1)
                    if there(j):
                        prod(j, t, 0)
                        if there(before[0]):
                            add(*before, 1)
                        delta(j, t, 0)
                    background(k, 2 * t)
                    if there(j):
                        outer(j, t, 0)
                        prod(j, t, 1)
                        add(j, t, 0)
                        delta(j, t, 1)
                        if there(before[0]):
                            times_q(*before)
                    background(k, 2 * t + 1)
                    if there(j):
                        outer(j, t, 1)

            for n in range(GD):
                gate_step(0, 0, n + 1)
            each_iteration(dve, iteration)


def kernel(L0_attn_x, L0_attn_W_in, L0_attn_W_k, L0_attn_W_v, L0_attn_W_q, L0_attn_W_beta, L0_attn_b_beta, L0_attn_W_out,
           L0_ffn_centroids, L0_ffn_expert_biases, L0_ffn_Ws_up, L0_ffn_Ws_down, L0_ffn_W_up, L0_ffn_W_down):
    import numpy as np
    import concourse.bacc as bacc
    from concourse.bass_utils import run_bass_kernel_spmd

    nc = bacc.Bacc("TRN2", target_bir_lowering=False, num_devices=1)
    laid_out = {
        "x": L0_attn_x, "w_in": L0_attn_W_in.T, "w_k": L0_attn_W_k.T, "w_v": L0_attn_W_v.T, "w_q": L0_attn_W_q.T,
        "w_beta": L0_attn_W_beta.T, "b_beta": L0_attn_b_beta.reshape(2, P).T, "w_out": L0_attn_W_out.T, "cent": L0_ffn_centroids.T,
        "ebias": L0_ffn_expert_biases, "ws_up": L0_ffn_Ws_up, "ws_down": L0_ffn_Ws_down, "w_up": L0_ffn_W_up,
        "w_down": L0_ffn_W_down,
    }
    arrays, args = {}, []
    for name, a in laid_out.items():
        a = np.ascontiguousarray(a)
        arrays[f"in_{name}"] = a
        args.append(nc.dram_tensor(f"in_{name}", a.shape, F32, kind="ExternalInput").ap())
    args.append(nc.dram_tensor("out_y", (B, T, D), F32, kind="ExternalOutput").ap())
    args.append(nc.dram_tensor("key_rows", (4, STEPS, G, W1), F32, kind="Internal").ap())
    args.append(nc.dram_tensor("query_rows", (4, STEPS, G, N), F32, kind="Internal").ap())
    macaron_program(nc, *args)
    r = run_bass_kernel_spmd(nc, [arrays], core_ids=[0])
    return r.results[0]["out_y"]
```
